# Optimizing a Trainium2 kernel written in Bass

```python
import numpy as np
import jax
import jax.numpy as jnp

def _softmax(x, axis=-1):
    return jax.nn.softmax(x, axis=axis)

def _gelu(x):
    return jax.nn.gelu(x, approximate=True)

def _silu(x):
    return jax.nn.silu(x)

def _sigmoid(x):
    return jax.nn.sigmoid(x)

def _layernorm(x, axis=-1, eps=1e-05):
    m = jnp.mean(x, axis=axis, keepdims=True)
    v = jnp.var(x, axis=axis, keepdims=True)
    return (x - m) / jnp.sqrt(v + eps)

def _scatter_add(tgt, idx, src, axis=0):
    return tgt.at[idx].add(src)

def _segment_sum(src, seg, n):
    return jax.ops.segment_sum(src, seg, n)
kernel_name = 'mk_flamingo_gated_d1_seqx_r2_1875bd'

def setup_inputs(seed: int=0):
    np.random.seed(seed)
    _w = jnp.asarray

    def _rec_inputs():
        import jax
        import jax.numpy as jnp
        _rk = jax.random.key(seed)
        x = -0.0002928 + 1 * jax.random.normal(jax.random.fold_in(_rk, 1), (2, 2048, 512), jnp.float32)
        _lenS = 2048 - jax.random.randint(jax.random.fold_in(_rk, 7), (2,), 0, max(1, 2048 // 4) + 1, jnp.int32)
        _lenS2 = 77 - jax.random.randint(jax.random.fold_in(_rk, 8), (2,), 0, max(1, 77 // 4) + 1, jnp.int32)
        _ctx_1024P = jax.random.normal(jax.random.fold_in(_rk, 11), (2, 16, 512), jnp.float32)
        _ctx_1024c = jax.random.dirichlet(jax.random.fold_in(_rk, 511), 0.3 * jnp.ones((16,), jnp.float32), (2, 77))
        _ctx_1024t = jnp.einsum('bsk,bkd->bsd', _ctx_1024c, _ctx_1024P)
        _ctx_1024t = _ctx_1024t * jax.lax.rsqrt(jnp.mean(jnp.square(_ctx_1024t)) + 1e-12) * 0.953939
        ctx_1024 = -1.39393e-06 + 0.999914 * (_ctx_1024t + 0.3 * jax.random.normal(jax.random.fold_in(_rk, 611), (2, 77, 512), jnp.float32))
        fside_BxS2_0 = 0.0132156 + 1.00766 * jax.random.normal(jax.random.fold_in(_rk, 12), (2, 77), jnp.float32)
        _validS = jnp.arange(2048)[None, :] < _lenS[:, None]
        _validS2 = jnp.arange(77)[None, :] < _lenS2[:, None]
        _causal = jnp.tril(jnp.ones((2048, 2048), dtype=bool))
        mask_BxS2_bk0 = jnp.logical_not(jnp.broadcast_to(_validS2[:, :], (2, 77)))
        _g = jax.random.normal(jax.random.fold_in(_rk, 9001), (2, 1), jnp.float32)
        _g = jnp.sign(_g) * jnp.maximum(jnp.abs(_g), 1.0) + (_g == 0) * 1.0
        g_xattn = _g[0]
        g_ffn = _g[1]
        return (x, ctx_1024, fside_BxS2_0, mask_BxS2_bk0, g_xattn, g_ffn)
    x, ctx_1024, fside_BxS2_0, mask_BxS2_bk0, g_xattn, g_ffn = _rec_inputs()

    def _L0_xattn_setup():
        import jax, jax.numpy as jnp
        import numpy as np
        EMBED_DIM = 512
        NUM_HEADS = 16
        HEAD_DIM = EMBED_DIM // NUM_HEADS
        B, SQ, SK = (2, 1024, 1024)
        key = jax.random.key(seed)
        ks = jax.random.split(key, 10)
        s = 1.0 / np.sqrt(EMBED_DIM)
        return {'tgt': jax.random.normal(ks[0], (B, SQ, EMBED_DIM), jnp.float32), 'mem': jax.random.normal(ks[1], (B, SK, EMBED_DIM), jnp.float32), 'attn_bias': jax.random.normal(ks[2], (B, SK), jnp.float32), 'memory_key_padding_mask': jax.random.randint(ks[3], (B, SK), 0, 2).astype(bool), 'Wq_w': jax.random.normal(ks[4], (EMBED_DIM, EMBED_DIM), jnp.float32) * s, 'Wq_b': jnp.zeros((EMBED_DIM,), jnp.float32), 'Wkv_w': jax.random.normal(ks[5], (2 * EMBED_DIM, EMBED_DIM), jnp.float32) * s, 'Wkv_b': jnp.zeros((2 * EMBED_DIM,), jnp.float32), 'out_w': jax.random.normal(ks[6], (EMBED_DIM, EMBED_DIM), jnp.float32) * s, 'out_b': jnp.zeros((EMBED_DIM,), jnp.float32)}
    _L0_xattn_all = _L0_xattn_setup()
    _L0_xattn_in = {k: v for k, v in _L0_xattn_all.items() if k in ('Wq_w', 'Wq_b', 'Wkv_w', 'Wkv_b', 'out_w', 'out_b')}
    del _L0_xattn_all

    def _L0_ffn_setup():
        import math
        import jax, jax.numpy as jnp
        import numpy as np
        B, L, D, F_FF, E = (4, 1024, 512, 2048, 8)
        TOP_K = 1
        CAPACITY_FACTOR = 1.25
        key = jax.random.key(seed)
        ks = jax.random.split(key, 4)
        h = jax.random.normal(ks[0], (B, L, D), dtype=jnp.float32)
        gate_w = jax.random.normal(ks[1], (E, D), dtype=jnp.float32) * 0.02
        gate_b = jnp.zeros((E,), dtype=jnp.float32)
        w1 = jax.random.normal(ks[2], (E, D, F_FF), dtype=jnp.float32) * 0.02
        b1 = jnp.zeros((E, F_FF), dtype=jnp.float32)
        w2 = jax.random.normal(ks[3], (E, F_FF, D), dtype=jnp.float32) * 0.02
        b2 = jnp.zeros((E, D), dtype=jnp.float32)
        return {'h': h, 'gate_w': gate_w, 'gate_b': gate_b, 'w1': w1, 'b1': b1, 'w2': w2, 'b2': b2}
    _L0_ffn_all = _L0_ffn_setup()
    _L0_ffn_in = {k: v for k, v in _L0_ffn_all.items() if k in ('gate_w', 'gate_b', 'w1', 'b1', 'w2', 'b2')}
    del _L0_ffn_all
    return {'x': x, 'ctx_1024': ctx_1024, 'fside_BxS2_0': fside_BxS2_0, 'mask_BxS2_bk0': mask_BxS2_bk0, 'g_xattn': g_xattn, 'g_ffn': g_ffn, 'L0_xattn_Wq_w': _L0_xattn_in['Wq_w'], 'L0_xattn_Wq_b': _L0_xattn_in['Wq_b'], 'L0_xattn_Wkv_w': _L0_xattn_in['Wkv_w'], 'L0_xattn_Wkv_b': _L0_xattn_in['Wkv_b'], 'L0_xattn_out_w': _L0_xattn_in['out_w'], 'L0_xattn_out_b': _L0_xattn_in['out_b'], 'L0_ffn_gate_w': _L0_ffn_in['gate_w'], 'L0_ffn_gate_b': _L0_ffn_in['gate_b'], 'L0_ffn_w1': _L0_ffn_in['w1'], 'L0_ffn_b1': _L0_ffn_in['b1'], 'L0_ffn_w2': _L0_ffn_in['w2'], 'L0_ffn_b2': _L0_ffn_in['b2']}

def reference(x, ctx_1024, fside_BxS2_0, mask_BxS2_bk0, g_xattn, g_ffn, L0_xattn_Wq_w, L0_xattn_Wq_b, L0_xattn_Wkv_w, L0_xattn_Wkv_b, L0_xattn_out_w, L0_xattn_out_b, L0_ffn_gate_w, L0_ffn_gate_b, L0_ffn_w1, L0_ffn_b1, L0_ffn_w2, L0_ffn_b2):
    import jax
    import jax.numpy as jnp

    def _L0_xattn_ref(tgt, mem, attn_bias, memory_key_padding_mask, Wq_w, Wq_b, Wkv_w, Wkv_b, out_w, out_b):
        import jax, jax.numpy as jnp
        import numpy as np
        EMBED_DIM = 512
        NUM_HEADS = 16
        HEAD_DIM = EMBED_DIM // NUM_HEADS
        B, SQ, SK = (2, 1024, 1024)
        b, sq, _ = tgt.shape
        sk = mem.shape[1]
        q = (tgt @ Wq_w.T + Wq_b).reshape(b, sq, NUM_HEADS, HEAD_DIM)
        kv = (mem @ Wkv_w.T + Wkv_b).reshape(b, sk, 2, NUM_HEADS, HEAD_DIM)
        k, v = (kv[:, :, 0], kv[:, :, 1])
        scale = 1.0 / np.sqrt(HEAD_DIM)
        scores = jnp.einsum('bthd,bshd->bhts', q, k * scale)
        scores = scores + attn_bias[:, None, None, :]
        pad = jnp.where(memory_key_padding_mask, 0.0, -jnp.inf).astype(scores.dtype)
        scores = scores + pad[:, None, None, :]
        attn = jax.nn.softmax(scores, axis=-1)
        ctx = jnp.einsum('bhts,bshd->bthd', attn, v)
        out = ctx.reshape(b, sq, EMBED_DIM) @ out_w.T + out_b
        return out

    def _L0_ffn_ref(h, gate_w, gate_b, w1, b1, w2, b2):
        import math
        import jax, jax.numpy as jnp
        import numpy as np
        B, L, D, F_FF, E = (4, 1024, 512, 2048, 8)
        TOP_K = 1
        CAPACITY_FACTOR = 1.25
        Bh, Lh, Dh = h.shape
        T = Bh * Lh
        capacity = max(1, math.ceil(CAPACITY_FACTOR * (T * TOP_K / E)))
        x = h.reshape(T, Dh)
        logits = x @ gate_w.T + gate_b
        probs = jax.nn.softmax(logits, axis=-1)
        idx = jnp.argmax(probs, axis=-1)
        top_prob = jnp.max(probs, axis=-1)
        one_hot = jax.nn.one_hot(idx, E, dtype=jnp.int32)
        pos = jnp.take_along_axis(jnp.cumsum(one_hot, axis=0), idx[:, None], axis=1)[:, 0] - 1
        keep = pos < capacity
        safe_pos = jnp.where(keep, pos, 0)
        buf = jnp.zeros((E, capacity, Dh), dtype=x.dtype)
        buf = buf.at[idx, safe_pos].add(x * keep[:, None].astype(x.dtype))
        hdn = jax.nn.relu(jnp.einsum('ecd,edf->ecf', buf, w1) + b1[:, None, :])
        eout = jnp.einsum('ecf,efd->ecd', hdn, w2) + b2[:, None, :]
        gathered = eout[idx, safe_pos]
        out = gathered * (top_prob * keep.astype(x.dtype))[:, None]
        return out.reshape(Bh, Lh, Dh)
    x = x + jnp.tanh(g_xattn[0]) * _L0_xattn_ref(_layernorm(x, axis=-1), ctx_1024, fside_BxS2_0, mask_BxS2_bk0, L0_xattn_Wq_w, L0_xattn_Wq_b, L0_xattn_Wkv_w, L0_xattn_Wkv_b, L0_xattn_out_w, L0_xattn_out_b)
    x = x + jnp.tanh(g_ffn[0]) * _L0_ffn_ref(_layernorm(x, axis=-1), L0_ffn_gate_w, L0_ffn_gate_b, L0_ffn_w1, L0_ffn_b1, L0_ffn_w2, L0_ffn_b2)
    return x

_drawn_inputs = setup_inputs


def setup_inputs(seed=0):
    import zlib

    import numpy as np

    out = dict(_drawn_inputs(seed))
    spreads = {'L0_xattn_Wq_b': (0.0, 0.382),
     'L0_xattn_Wkv_b': (0.0, 0.1),
     'L0_xattn_out_b': (0.0, 0.1),
     'L0_ffn_gate_b': (0.0, 0.1),
     'L0_ffn_b1': (0.0, 0.751),
     'L0_ffn_b2': (0.0, 0.463)}
    factors = {}
    for name, (base, spread) in spreads.items():
        noise = np.random.default_rng([zlib.crc32(name.encode()), seed]).standard_normal(out[name].shape)
        drawn = base * np.exp(spread * noise) if base else spread * noise
        out[name] = jnp.asarray(drawn.astype(out[name].dtype))
    for name, factor in factors.items():
        out[name] = (out[name] * factor).astype(out[name].dtype)
    return out
```

```python
from contextlib import ExitStack

import concourse.bass as bass
from concourse import mybir

F32 = mybir.dt.float32
F32R = mybir.dt.float32r
I32 = mybir.dt.int32
U8 = mybir.dt.uint8
ALU = mybir.AluOpType
ACT = mybir.ActivationFunctionType
AX = mybir.AxisListType.X

P = 128
BATCH, SEQ, D = 2, 2048, 512
KEYS = 77
HEADS, HD = 16, 32
TOK = BATCH * SEQ
DC = D // P
QH = HEADS // DC
QK = QH * KEYS
KCH = [P, P, QK - 2 * P]
GT = 2
GTOK = GT * P
GROUPS = TOK // GTOK
NE, FF = 8, 2048
CAP = 640
NB = CAP // P
FQ = FF // 512
ROW = D + 4
C_RSTD, C_NMR, C_SCALE, C_TOK = D, D + 1, D + 2, D + 3
EPS = 1e-5
PADDED = -1e30
NO_TOKEN = TOK
DROPPED = 16384.0

TP_USES = [("PT", -1, 0), ("PT", -1, 1), ("PT", -1, 2), ("PT", -1, 3), ("XT", 1, 0), ("XT", 1, 1),
           ("PT", -1, 4), ("H2T", -2, 0), ("PT", -1, 5), ("H2T", -2, 1)]
ACC_USES = [("AV", -1, 0), ("Q", 1, 0), ("Q", 1, 1), ("AV", -1, 1), ("GATE", -2, 0), ("O", -1, 0), ("O", -1, 1),
            ("CUM", -2, 0)]


def number_uses(uses):
    at, n = {}, 0
    for body in range(-1, GROUPS + 2):
        for stage, shift, part in uses:
            if 0 <= body + shift < GROUPS:
                at[(body, stage, part)] = n
                n += 1
    return at


RINGS = {"tp": (number_uses(TP_USES), len(TP_USES)), "acc": (number_uses(ACC_USES), len(ACC_USES))}


def is_fixed(I):
    return isinstance(I[0], int)


def num(I, shift=0):
    return I[0] * 2 + (I[1] + shift)


def par(I, shift=0):
    return (I[1] + shift) % 2


def has(I, shift):
    return not is_fixed(I) or 0 <= num(I, shift) < GROUPS


def ring_use(ring, I, stage, part):
    table, per_body = RINGS[ring]
    if is_fixed(I):
        n = table[(num(I), stage, part)]
        return n % 2, n // 2
    n = table[(2 + I[1], stage, part)]
    return n % 2, (I[0] - 1) * per_body + n // 2


def use_before(ring, I, stage, part):
    table, _ = RINGS[ring]
    body = num(I) if is_fixed(I) else 4 + I[1]
    n = table[(body, stage, part)]
    for (b, st, pt), m in table.items():
        if m == n - 2:
            shift = next(x[1] for x in TP_USES + ACC_USES if x[0] == st)
            return st, pt, num(I, b - body + shift)
    return None


def attend_bodies(eng, body):
    for b in (-1, 0, 1):
        body((b // 2, b % 2), 0, 0)
    with eng.Fori(1, 4) as h:
        body((h, 0), 0, 0)
        body((h, 1), 0, 0)
    body((4, 0), 1, 0)
    body((4, 1), 1, 1)
    with eng.Fori(5, 7) as h:
        body((h, 0), 1, 1)
        body((h, 1), 1, 1)
    for b in range(14, GROUPS + 2):
        body((b // 2, b % 2), 1, 1)


def wait(eng, sem, value):
    if not isinstance(value, int) or value > 0:
        eng.wait_ge(sem, value)


SETUP = ([("wT", w, c) for w in range(4) for c in range(DC)]
         + [("b1", 0, 0), ("bias", 0, 0), ("gw", 0, 0), ("cx", 0, 0), ("cx", 1, 0)]
         + [("k", m, 0) for m in range(DC)] + [("v", b, 0) for b in range(BATCH)]
         + [("vb", b, r) for b in range(BATCH) for r in range(3)])
AT_SETUP = {use: n for n, use in enumerate(SETUP)}
VB_PIECES = [[(0, 0), (1, 0)], [(1, 1), (2, 1)], [(3, 1), (3, 2)]]
GATE_STEPS, ROUTE_STEPS = 6, 3
POOL_CONSTS = 7
N_SIDES = 10


def flamingo_block(nc, x, ctx_in, fside, mask, g_xattn, g_ffn, wq, bq, wkv, bkv, wo, bo,
                   gate_w, gate_b, w1, b1, w2, b2, out):
    x_rows = x.rearrange("b s d -> (b s) d").rearrange("(t p) d -> p t d", p=P)
    out_flat = out.rearrange("b s d -> (b s) d")
    out_rows = out_flat.rearrange("(t p) d -> p t d", p=P)
    slots = nc.dram_tensor("dispatched_rows", (NE * CAP, ROW), F32, kind="Internal").ap()
    slot_blocks = slots.rearrange("(t p) d -> p t d", p=P)

    es = ExitStack()
    with es:
        def sem(name):
            return es.enter_context(nc.semaphore(name))

        def sb(name, shape, dt=F32, stack=None):
            return (stack or es).enter_context(nc.sbuf_tensor(name, shape, dt))

        ident = sb("ident", [P, P])
        ones = sb("ones", [P, P])
        tri = sb("tri", [P, P])
        raw1 = [sb(f"raw_w1_{i}", [P, DC, 512]) for i in range(2)]
        raw2 = [sb(f"raw_w2_{i}", [P, DC, 512]) for i in range(2)]
        b1T = sb("b1T", [P, NE * FF // P])
        plan = sb("plan", [1, 32], I32)
        plan_f = sb("plan_f", [1, 32])

        tp = [es.enter_context(nc.psum_tensor(f"tp{i}", [P, 512], F32)) for i in range(2)]
        acc = [es.enter_context(nc.psum_tensor(f"acc{i}", [P, 512], F32)) for i in range(2)]
        sc = [es.enter_context(nc.psum_tensor(f"sc{i}", [P, 2, 512], F32)) for i in range(2)]

        ea = ExitStack()
        A = lambda name, shape, dt=F32: sb(name, shape, dt, ea)
        WqT = [A(f"WqT{i}", [P, DC, D], F32R) for i in "hl"]
        WoT = [A(f"WoT{i}", [P, DC, D], F32R) for i in "hl"]
        KB = [A(f"KB{i}", [P, BATCH, DC, QK], F32R) for i in "hl"]
        VB = [A(f"VB{i}", [P, BATCH, DC, 3, P], F32R) for i in "hl"]
        xnT = [A(f"xnT{i}", [P, DC, GTOK], F32R) for i in "hl"]
        qT = [A(f"qT{i}", [P, DC, GTOK], F32R) for i in "hl"]
        ctxT = [A(f"ctxT{i}", [P, DC, GTOK], F32R) for i in "hl"]
        PT = [[A(f"PT{p}{i}", [P, 3, 512], F32R) for i in "hl"] for p in range(2)]
        s = [A(f"s{i}", [P, GT, HEADS * KEYS]) for i in range(2)]
        x_in = [A(f"x_in{i}", [P, GT, D]) for i in range(2)]
        row = [A(f"row{i}", [P, GT, ROW]) for i in range(2)]
        h2 = A("h2", [P, GT, D])
        h2T = A("h2T", [P, DC, GTOK])
        tgbo = A("tgbo", [P, D])
        bias = A("bias", [P, BATCH, KEYS])
        wide = A("wide", [KEYS, 320])
        keys = A("keys", [P, 2, BATCH])
        qmask = A("qmask", [P, QH])
        ktmp = A("ktmp", [P, BATCH * KEYS])
        biasT = A("biasT", [P, 3 * DC])
        bqT, bkT, bvT = (biasT[:, i * DC:(i + 1) * DC] for i in range(3))
        gwT = A("gwT", [P, DC, NE])
        gb = A("gb", [P, NE])
        gin = A("gin", [P, 2])
        gt = A("gt", [P, 2])
        eoff = A("eoff", [P, GT, NE])
        rank = A("rank", [P, GT, NE])
        over = A("over", [P, GT, NE])
        mhalf = A("mhalf", [P, GT])
        mx = [A(f"mx{i}", [P, GT, HEADS]) for i in range(2)]
        den = [A(f"den{i}", [P, GT, HEADS]) for i in range(2)]
        rden = [A(f"rden{i}", [P, GT, HEADS]) for i in range(2)]
        st1 = A("st1", [P, GT, 6])
        mv1 = A("mv1", [P, GT, 2])
        ve1 = A("ve1", [P, GT])
        rs1 = A("rs1", [P, GT])
        nm1 = A("nm1", [P, GT])
        nmr1 = A("nmr1", [P, GT])
        st2 = A("st2", [P, GT, 6])
        mv2 = A("mv2", [P, GT, 2])
        ve2 = A("ve2", [P, GT])
        nm2 = A("nm2", [P, GT])
        lg = A("lg", [P, GT, NE])
        lmx = A("lmx", [P, GT])
        lm = A("lm", [P, GT, NE])
        ex = A("ex", [P, GT, NE])
        wr = A("wr", [P, GT, NE])
        wm = A("wm", [P, GT])
        oh = A("oh", [P, GT, NE])
        pre = A("pre", [P, GT, NE])
        run = A("run", [P, NE])
        cs = A("cs", [P, GT, NE])
        cu = A("cu", [P, GT, NE])
        cv = A("cv", [P, GT, NE])
        cw = A("cw", [P, GT, NE])
        slot = A("slot", [P, GT], I32)
        exs = A("exs", [P, GT])
        exr = A("exr", [P, GT])
        tokf = A("tokf", [P, GT])
        wkT, wvT = s[0][:, :, :].rearrange("p t k -> p (t k)")[:, 0:DC * D].rearrange("p (c n) -> p c n", c=DC), \
            s[1][:, :, :].rearrange("p t k -> p (t k)")[:, 0:DC * D].rearrange("p (c n) -> p c n", c=DC)
        cx_rows = x_in[0]
        cxT = h2T[:, :, 0:BATCH * KEYS]
        v_rows = h2
        empty = row[0][:, 0, :]
        raw_q, raw_k, raw_v, raw_o = raw1[0], raw1[1], raw2[0], raw2[1]
        b1_rows = x_in[1][:, 0, 0:P]
        gw_rows = x_in[1][0:NE, 1, :]
        bias_rows = x_in[1][0:3 * DC, 0, P:2 * P]
        fside_b = row[1][:, 0, 0:BATCH * KEYS].rearrange("p (b k) -> p b k", b=BATCH)
        mask_b = row[1][:, 1, 0:D].bitcast(U8)[:, 0:BATCH * KEYS].rearrange("p (b k) -> p b k", b=BATCH)
        ea.close()

        eb = es.enter_context(ExitStack())
        B = lambda name, shape, dt=F32: sb(name, shape, dt, eb)
        W1 = [[B(f"W1{u}{i}", [P, DC, 512], F32R) for i in "hl"] for u in range(2)]
        W2 = [[B(f"W2{u}{i}", [P, DC, 512], F32R) for i in "hl"] for u in range(2)]
        xr = [B(f"xr{i}", [P, NB, ROW]) for i in range(2)]
        hB = [B(f"hB{i}", [P, D]) for i in range(2)]
        hBT = [[B(f"hBT{p}{i}", [P, NB, DC, P], F32R) for i in "hl"] for p in range(2)]
        g1s = [B(f"g1s{i}", [P, 512]) for i in range(2)]
        hid = [B(f"hid{i}", [P, DC, P]) for i in range(2)]
        hidT = [[B(f"hidT{p}{i}", [P, DC, P], F32R) for i in "hl"] for p in range(2)]
        yo = [B(f"yo{i}", [P, D]) for i in range(2)]
        b2b = [B(f"b2b{i}", [P, D]) for i in range(2)]
        oacc = [acc[0][:, :], acc[1][:, :], sc[0][:, 0, :], sc[0][:, 1, :], sc[1][:, 0, :]]
        g1p = [sc[1][:, 1, :], tp[1][:, :]]
        tb = tp[0]

        waits_passed = sem("waits_passed")
        consts_made = sem("consts_made")
        sides_loaded = sem("sides_loaded")
        raw_loaded = [sem(f"raw_loaded{i}") for i in range(4)]
        ctx_loaded = sem("ctx_loaded")
        empty_made = sem("empty_made")
        slots_cleared = sem("slots_cleared")
        setup_full = sem("setup_full")
        setup_hi = sem("setup_hi")
        setup_free = sem("setup_free")
        gates_made = sem("gates_made")
        small_step = sem("small_step")
        tgbo_made = sem("tgbo_made")
        kb_hi = sem("kb_hi")
        kb_done = sem("kb_done")
        tp_full = [sem(f"tp_full{i}") for i in range(2)]
        tp_free = [sem(f"tp_free{i}") for i in range(2)]
        acc_full = [sem(f"acc_full{i}") for i in range(2)]
        acc_free = [sem(f"acc_free{i}") for i in range(2)]
        sc_full = [sem(f"sc_full{i}") for i in range(2)]
        sc_free = [sem(f"sc_free{i}") for i in range(2)]
        x_loaded = [sem(f"x_loaded{i}") for i in range(2)]
        row_loaded = [sem(f"row_loaded{i}") for i in range(2)]
        stats1 = sem("stats1")
        var1 = sem("var1")
        scaled1 = sem("scaled1")
        xn_ready = sem("xn_ready")
        xnT_hi = sem("xnT_hi")
        xnT_ready = sem("xnT_ready")
        q_hi = sem("q_hi")
        q_ready = sem("q_ready")
        s_biased = sem("s_biased")
        max_ready = sem("max_ready")
        s_shifted = sem("s_shifted")
        exp_ready = sem("exp_ready")
        den_ready = sem("den_ready")
        rden_ready = sem("rden_ready")
        p_ready = sem("p_ready")
        pt_hi = sem("pt_hi")
        pt_ready = sem("pt_ready")
        ctx_hi = sem("ctx_hi")
        ctx_ready = sem("ctx_ready")
        phase_b = sem("phase_b")
        row_based = sem("row_based")
        x1_ready = sem("x1_ready")
        stats2 = sem("stats2")
        var2 = sem("var2")
        scaled2 = sem("scaled2")
        h2_ready = sem("h2_ready")
        h2T_ready = sem("h2T_ready")
        gate_step = sem("gate_step")
        gate_exp = sem("gate_exp")
        route_step = sem("route_step")
        cum_read = sem("cum_read")
        slot_mixed = sem("slot_mixed")
        slot_ready = sem("slot_ready")
        top_ready = sem("top_ready")
        row_ready = sem("row_ready")
        row_scattered = [sem(f"row_scattered{i}") for i in range(2)]
        out_stored = [sem(f"out_stored{i}") for i in range(2)]
        plan_ready = sem("plan_ready")
        count_ready = sem("count_ready")
        xr_loaded = [sem(f"xr_loaded{i}") for i in range(2)]
        b2_loaded = [sem(f"b2_loaded{i}") for i in range(2)]
        w1_loaded = [sem(f"w1_loaded{i}") for i in range(2)]
        w2_loaded = [sem(f"w2_loaded{i}") for i in range(2)]
        w1_hi = sem("w1_hi")
        w2_hi = sem("w2_hi")
        w1_ready = sem("w1_ready")
        w2_ready = sem("w2_ready")
        hB_ready = sem("hB_ready")
        hBT_full = sem("hBT_full")
        hBT_hi = sem("hBT_hi")
        hBT_ready = sem("hBT_ready")
        g1_full = sem("g1_full")
        g1_out = sem("g1_out")
        hid_full = sem("hid_full")
        hid_ready = sem("hid_ready")
        hidT_hi = sem("hidT_hi")
        hidT_ready = sem("hidT_ready")
        g2_done = sem("g2_done")
        y_added = sem("y_added")
        y_ready = sem("y_ready")
        y_scattered = sem("y_scattered")

        def sbank(n):
            return sc[(n // 2) % 2][:, n % 2, :]

        def load_unit(eng, e, fq, i):
            eng.dma_start(raw1[i][:, :, :], w1.rearrange("e (c p) f -> p (e c) f", p=P)[
                :, bass.ds(e * DC, DC), fq * 512:(fq + 1) * 512]).then_inc(w1_loaded[i], 16)
            eng.dma_start(raw2[i][:, :, :], w2.rearrange("e (c p) n -> p (e c) n", p=P)[
                :, bass.ds(e * (FF // P) + fq * DC, DC), :]).then_inc(w2_loaded[i], 16)

        def next_of(e):
            return nc.s_assert_within(e + 1, 1, NE - 1, skip_runtime_bounds_check_because="not for the last expert")

        def load_rows(eng, e, i):
            eng.dma_start(xr[i][:, :, :], slot_blocks[:, bass.ds(e * NB, NB), :]).then_inc(xr_loaded[i], 16)
            eng.dma_start(b2b[i][:, :], b2[bass.ds(e, 1), :].to_broadcast([P, D])).then_inc(b2_loaded[i], 16)

        def blocks_of(eng, e, shift=0):
            return eng.value_load(plan[0:1, bass.ds(e + shift, 1)], min_val=0, max_val=NB)

        def blocks_before(eng, e, shift=0):
            return eng.value_load(plan[0:1, bass.ds(e + (NE + 1 + shift), 1)], min_val=0, max_val=NE * NB)

        def per_block(eng, n, b, work):
            if b == 0:
                work(0)
            else:
                with eng.If(n > b):
                    work(b)

        def stand_alone(eng):
            eng.sem_inc(waits_passed, 1)

        block = es.enter_context(nc.Block())

        @block.sync
        def _(sp):
            sp.dma_start(raw_q[:, :, :], wq.rearrange("(m p) k -> p m k", p=P)).then_inc(raw_loaded[0], 16)
            sp.dma_start(cx_rows[0:KEYS, :, :], ctx_in.rearrange("b s d -> s b d")).then_inc(ctx_loaded, 16)
            wkv_v = wkv.rearrange("(m p) k -> p m k", p=P)
            sp.dma_start(raw_k[:, :, :], wkv_v[:, 0:DC, :]).then_inc(raw_loaded[1], 16)
            sp.dma_start(raw_v[:, :, :], wkv_v[:, DC:2 * DC, :]).then_inc(raw_loaded[2], 16)
            sp.dma_start(raw_o[:, :, :], wo.rearrange("(m p) k -> p m k", p=P)).then_inc(raw_loaded[3], 16)
            sp.wait_ge(setup_free, AT_SETUP[("cx", 1, 0)] + 1)
            for i in range(2):
                sp.dma_start(x_in[i][:, :, :], x_rows[:, GT * i:GT * (i + 1), :]).then_inc(x_loaded[i], 16)
            sp.wait_ge(empty_made, 2)
            sp.dma_start(slot_blocks, empty.unsqueeze(1).to_broadcast([P, NE * NB, ROW])).then_inc(slots_cleared, 16)
            for i in range(2):
                load_unit(sp, 0, i, i)

            def body(I, batch, batch1):
                if has(I, -1):
                    before = I[0] + (I[1] - 1) // 2
                    if is_fixed(I) and before == 0:
                        sp.wait_ge(slots_cleared, 16)
                    wait(sp, row_scattered[par(I, -1)], before * 32)
                    stand_alone(sp)
                    wait(sp, out_stored[par(I, -1)], before * 16)
                    stand_alone(sp)
                    sp.dma_start(row[par(I, -1)][:, :, 0:D],
                                 x_rows[:, bass.ds(num(I, -1) * GT, GT), :]).then_inc(row_loaded[par(I, -1)], 16)
                if has(I, 2) and has(I, 0):
                    before = (I[0] + (I[1] - 1) // 2, par(I, -1))
                    bank, n = ring_use("tp", before, "XT", 1)
                    sp.wait_ge(tp_full[bank], n + 1)
                    stand_alone(sp)
                    sp.dma_start(x_in[par(I)][:, :, :],
                                 x_rows[:, bass.ds(num(I, 2) * GT, GT), :]).then_inc(x_loaded[par(I)], 16)
                if has(I, -1):
                    sp.wait_ge(x1_ready, num(I, -1) * 2 + 2)
                    stand_alone(sp)
                    sp.dma_start(out_rows[:, bass.ds(num(I, -1) * GT, GT), :],
                                 row[par(I, -1)][:, :, 0:D]).then_inc(out_stored[par(I, -1)], 16)

            attend_bodies(sp, body)

            for i in range(2):
                sp.wait_ge(out_stored[i], 16 * GROUPS // 2)
                sp.wait_ge(row_scattered[i], 32 * GROUPS // 2)
            sp.wait_ge(plan_ready, 1)
            sp.sem_inc(phase_b, 1)
            load_rows(sp, 0, 0)
            with sp.Fori(0, NE // 2) as it:
                for odd in range(2):
                    e = it * 2 + odd
                    sp.wait_ge(y_scattered, blocks_before(sp, e) * 16)
                    stand_alone(sp)
                    if odd == 0:
                        load_rows(sp, e + 1, 1)
                    else:
                        with sp.If(it < NE // 2 - 1):
                            load_rows(sp, next_of(e), 0)
                    for fq in range(FQ):
                        def next_unit():
                            sp.wait_ge(w1_ready, e * FQ + (fq + 1))
                            sp.wait_ge(w2_ready, e * FQ + (fq + 1))
                            stand_alone(sp)
                            load_unit(sp, e if fq < 2 else next_of(e), (fq + 2) % FQ, fq % 2)
                        if odd == 1 and fq >= 2:
                            with sp.If(it < NE // 2 - 1):
                                next_unit()
                        else:
                            next_unit()

        @block.gpsimd
        def _(pool):
            def const(ins):
                ins.then_inc(consts_made, 1)
                const.n += 1
                pool.wait_ge(consts_made, const.n)
            const.n = 0

            const(pool.memset(ident[:, :], 0.0))
            const(pool.affine_select(ident[:, :], ident[:, :], [[-1, P]], ALU.not_equal, 1.0, base=0,
                                     channel_multiplier=1))
            const(pool.memset(ones[:, :], 1.0))
            const(pool.memset(wide[:, :], 0.0))
            const(pool.affine_select(wide[:, :], wide[:, :], [[1, 320]], ALU.not_equal, 1.0, base=-P,
                                     channel_multiplier=-1))
            for part in VB:
                const(pool.memset(part[:, :, :, :, :].bitcast(F32), 0.0))
            assert const.n == POOL_CONSTS
            pool.memset(empty, 0.0).then_inc(empty_made, 1)
            pool.wait_ge(empty_made, 1)
            pool.memset(empty[:, C_TOK:C_TOK + 1].bitcast(I32), NO_TOKEN).then_inc(empty_made, 1)
            const(pool.affine_select(tri[:, :], ones[:, :], [[1, P]], ALU.is_ge, 0.0, base=0,
                                     channel_multiplier=-1))
            const(pool.iota(tokf[:, :], [[P, GT]], base=0, channel_multiplier=1,
                            allow_small_or_imprecise_dtypes=True))
            const(pool.memset(mhalf[:, :], -0.5))
            const(pool.memset(run[:, :], 0.0))
            pool.wait_ge(tgbo_made, 1)

            def norm_scale(g, mv, ve, rstd, nm, nmr, var, scaled):
                pool.wait_ge(var, g + 1)
                pool.tensor_tensor(rstd, ve[:, :], mhalf[:, :], ALU.pow).then_inc(scaled, 1)
                pool.wait_ge(scaled, g * 3 + 1)
                pool.tensor_tensor(nm[:, :], mv[:, :, 0], rstd, ALU.mult).then_inc(scaled, 1)
                pool.wait_ge(scaled, g * 3 + 2)
                stand_alone(pool)
                pool.tensor_scalar(nmr, nm[:, :], -1.0, None, ALU.mult).then_inc(scaled, 1)

            def scale1(g, p):
                wait(pool, xn_ready, g * 2)
                norm_scale(g, mv1, ve1, rs1[:, :], nm1, nmr1[:, :], var1, scaled1)

            scale1(0, 0)

            def body(I, batch, batch1):
                g, p = num(I), par(I)
                if has(I, 0):
                    for t in range(GT):
                        st = s[p][:, t, :].rearrange("p (h k) -> p h k", h=HEADS)
                        pool.wait_ge(max_ready, g * 2 + (t + 1))
                        pool.tensor_tensor(st, st, mx[p][:, t, :].unsqueeze(2).to_broadcast([P, HEADS, KEYS]),
                                           ALU.subtract).then_inc(s_shifted, 1)
                if has(I, 0):
                    for t in range(GT):
                        st = s[p][:, t, :].rearrange("p (h k) -> p h k", h=HEADS)
                        pool.wait_ge(rden_ready, g * 2 + (t + 1))
                        pool.tensor_tensor(st, st, rden[p][:, t, :].unsqueeze(2).to_broadcast([P, HEADS, KEYS]),
                                           ALU.mult).then_inc(p_ready, 1)
                if has(I, -1):
                    g1, p1 = num(I, -1), par(I, -1)
                    pool.wait_ge(row_loaded[p1], (I[0] + (I[1] - 1) // 2) * 16 + 16)
                    for t in range(GT):
                        r = row[p1][:, t, 0:D]
                        pool.tensor_tensor(r, r, tgbo[:, :], ALU.add).then_inc(row_based, 1)
                if has(I, -2):
                    g2 = num(I, -2)
                    pool.wait_ge(gate_step, g2 * GATE_STEPS + GATE_STEPS)
                    wait(pool, cum_read, g2 * 2)
                    wait(pool, route_step, g2 * ROUTE_STEPS)
                    stand_alone(pool)
                    pool.tensor_copy(pre[:, 0, :], run[:, :]).then_inc(route_step, 1)
                    pool.tensor_tensor(pre[:, 1, :], run[:, :], oh[:, 0, :], ALU.add).then_inc(route_step, 1)
                    pool.wait_ge(route_step, g2 * ROUTE_STEPS + 2)
                    pool.tensor_tensor(run[:, :], pre[:, 1, :], oh[:, 1, :], ALU.add).then_inc(route_step, 1)
                if has(I, -2):
                    g2, p2 = num(I, -2), par(I, -2)
                    pool.wait_ge(cum_read, g2 * 2 + 2)
                    pool.tensor_tensor(cv[:, :, :], cs[:, :, :], cu[:, :, :], ALU.add).then_inc(slot_mixed, 1)
                    pool.wait_ge(slot_mixed, g2 * 2 + 1)
                    wait(pool, slot_ready, g2)
                    pool.tensor_tensor(cw[:, :, :], cv[:, :, :], oh[:, :, :], ALU.mult).then_inc(slot_mixed, 1)
                if has(I, -1):
                    g1, p1 = num(I, -1), par(I, -1)
                    norm_scale(g1, mv2, ve2, row[p1][:, :, C_RSTD], nm2, row[p1][:, :, C_NMR], var2, scaled2)
                if has(I, 2):
                    scale1(num(I, 2), par(I, 2))
                if has(I, -2):
                    pool.wait_ge(top_ready, g2 * 2 + 2)
                    stand_alone(pool)
                    pool.tensor_scalar(row[p2][:, :, C_SCALE], exr[:, :], gt[:, 1:2], None,
                                       ALU.mult).then_inc(row_ready, 1)
                    pool.tensor_copy(row[p2][:, :, C_TOK].bitcast(I32), tokf[:, :]).then_inc(row_ready, 1)
                    pool.wait_ge(row_ready, g2 * 3 + 2)
                    stand_alone(pool)
                    pool.tensor_scalar(tokf[:, :], tokf[:, :], float(GTOK), None, ALU.add).then_inc(row_ready, 1)
                    pool.wait_ge(row_ready, g2 * 3 + 3)
                    pool.wait_ge(slot_ready, g2 + 1)
                    stand_alone(pool)
                    for t in range(GT):
                        pool.indirect_dma_start(
                            slots, bass.IndirectOffsetOnAxis(ap=slot[:, t:t + 1], axis=0), row[p2][:, t, :], None,
                            bounds_check=NE * CAP - 1, oob_is_err=False).then_inc(row_scattered[p2], 16)

            attend_bodies(pool, body)

            pool.wait_ge(phase_b, 1)
            with pool.Fori(0, NE // 2) as it:
                for odd in range(2):
                    e = it * 2 + odd
                    n, first = blocks_of(pool, e), blocks_before(pool, e)

                    def scatter(b):
                        pool.wait_ge(y_ready, first + (b + 1))
                        stand_alone(pool)
                        pool.indirect_dma_start(
                            out_flat, bass.IndirectOffsetOnAxis(ap=xr[odd][:, b, C_TOK:C_TOK + 1].bitcast(I32), axis=0),
                            yo[b % 2][:, :], None, bounds_check=TOK - 1, oob_is_err=False).then_inc(y_scattered, 16)
                        pool.wait_ge(y_scattered, first * 16 + (b + 1) * 16)
                        stand_alone(pool)

                    for b in range(NB):
                        per_block(pool, n, b, scatter)

        @block.scalar
        def _(act):
            for dst, src in (
                (b1_rows, b1.rearrange("e (c p) -> (e c) p", p=P)),
                (gw_rows, gate_w),
                (bias_rows[0:DC, :], bq.rearrange("(m p) -> m p", p=P)),
                (bias_rows[DC:3 * DC, :], bkv.rearrange("(m p) -> m p", p=P)),
                (gb[:, :], gate_b.unsqueeze(0).to_broadcast([P, NE])),
                (tgbo[:, :], bo.unsqueeze(0).to_broadcast([P, D])),
                (fside_b, fside.unsqueeze(0).to_broadcast([P, BATCH, KEYS])),
                (mask_b, mask.unsqueeze(0).to_broadcast([P, BATCH, KEYS])),
                (gin[:, 0:1], g_xattn.unsqueeze(0).to_broadcast([P, 1])),
                (gin[:, 1:2], g_ffn.unsqueeze(0).to_broadcast([P, 1])),
            ):
                act.dma_start(dst, src).then_inc(sides_loaded, 16)
            act.wait_ge(sides_loaded, 16 * N_SIDES)
            act.activation(gt[:, :], gin[:, :], ACT.Tanh).then_inc(gates_made, 1)

            for n, (what, w, c) in enumerate(SETUP):
                if what == "wT" and w in (0, 3):
                    act.wait_ge(setup_full, n + 1)
                    act.activation((WqT if w == 0 else WoT)[0][:, c, :], sbank(n), ACT.Copy).then_inc(setup_hi, 1)
                elif what == "vb":
                    act.wait_ge(setup_full, n + 1)
                    act.wait_ge(consts_made, POOL_CONSTS)
                    for q, (hh, j) in enumerate(VB_PIECES[c]):
                        act.activation(VB[0][:, w, :, j, hh * HD:(hh + 1) * HD],
                                       sbank(n)[:, q * P:(q + 1) * P].rearrange("p (m d) -> p m d", m=DC),
                                       ACT.Copy).then_inc(setup_hi, 1)

            def normalise1(g, p):
                act.wait_ge(scaled1, g * 3 + 3)
                for t in range(GT):
                    act.activation(x_in[p][:, t, :], x_in[p][:, t, :], ACT.Identity, bias=nmr1[:, t:t + 1],
                                   scale=rs1[:, t:t + 1]).then_inc(xn_ready, 1)

            def body(I, batch, batch1):
                g, p = num(I), par(I)

                def pt_upper(j):
                    if not has(I, -1):
                        return
                    bank, n = ring_use("tp", I, "PT", j)
                    rows = P if j % 3 < 2 else KCH[2]
                    act.wait_ge(tp_full[bank], n + 1)
                    act.activation(PT[j // 3][0][0:rows, j % 3, :], tp[bank][0:rows, :], ACT.Copy).then_inc(pt_hi, 1)

                def exponentials(t):
                    if not has(I, 0):
                        return
                    act.wait_ge(s_shifted, g * 2 + (t + 1))
                    act.activation(s[p][:, t, :], s[p][:, t, :], ACT.Exp).then_inc(exp_ready, 1)

                def xnT_upper(j):
                    if not has(I, 1):
                        return
                    bank, n = ring_use("tp", I, "XT", j)
                    act.wait_ge(tp_full[bank], n + 1)
                    act.activation(xnT[0][:, 2 * j:2 * j + 2, :],
                                   tp[bank][:, :].rearrange("p (c k) -> p c k", c=2), ACT.Copy).then_inc(xnT_hi, 1)

                def h2T_copy(j):
                    if not has(I, -2):
                        return
                    bank, n = ring_use("tp", I, "H2T", j)
                    act.wait_ge(tp_full[bank], n + 1)
                    act.activation(h2T[:, 2 * j:2 * j + 2, :], tp[bank][:, :].rearrange("p (c k) -> p c k", c=2),
                                   ACT.Copy).then_inc(h2T_ready, 1)

                def ctx_upper(q):
                    if not has(I, -1):
                        return
                    bank, n = ring_use("acc", I, "AV", q)
                    act.wait_ge(acc_full[bank], n + 1)
                    for mm in range(2):
                        m = 2 * q + mm
                        act.activation(ctxT[0][:, m, :], acc[bank][:, mm * GTOK:(mm + 1) * GTOK], ACT.Identity,
                                       bias=bvT[:, m:m + 1]).then_inc(ctx_hi, 1)

                def q_upper(q):
                    if not has(I, 1):
                        return
                    bank, n = ring_use("acc", I, "Q", q)
                    act.wait_ge(acc_full[bank], n + 1)
                    for mm in range(2):
                        m = 2 * q + mm
                        act.activation(qT[0][:, m, :], acc[bank][:, mm * GTOK:(mm + 1) * GTOK], ACT.Identity,
                                       bias=bqT[:, m:m + 1]).then_inc(q_hi, 1)

                def normalise2():
                    if not has(I, -2):
                        return
                    g2, p2 = num(I, -2), par(I, -2)
                    act.wait_ge(scaled2, g2 * 3 + 3)
                    for t in range(GT):
                        act.activation(h2[:, t, :], row[p2][:, t, 0:D], ACT.Identity,
                                       bias=row[p2][:, t, C_NMR:C_NMR + 1],
                                       scale=row[p2][:, t, C_RSTD:C_RSTD + 1]).then_inc(h2_ready, 1)

                pt_upper(0)
                if has(I, 1):
                    normalise1(num(I, 1), par(I, 1))
                pt_upper(1)
                pt_upper(2)
                pt_upper(3)
                normalise2()
                xnT_upper(0)
                ctx_upper(0)
                xnT_upper(1)
                exponentials(0)
                pt_upper(4)
                h2T_copy(0)
                pt_upper(5)
                q_upper(0)
                h2T_copy(1)
                exponentials(1)
                q_upper(1)
                ctx_upper(1)
                if has(I, -2):
                    act.wait_ge(gate_step, num(I, -2) * GATE_STEPS + 3)
                    act.activation(ex[:, :, :], lm[:, :, :], ACT.Exp).then_inc(gate_exp, 1)

            attend_bodies(act, body)

            act.wait_ge(phase_b, 1)

            def split1(i, count, loads):
                act.wait_ge(w1_loaded[i], loads)
                act.activation(W1[i][0][:, :, :], raw1[i][:, :, :], ACT.Copy).then_inc(w1_hi, 1)

            def split2(i, count, loads):
                act.wait_ge(w2_loaded[i], loads)
                act.activation(W2[i][0][:, :, :], raw2[i][:, :, :], ACT.Copy).then_inc(w2_hi, 1)

            def normalise(odd, loads, first, j):
                act.wait_ge(xr_loaded[odd], loads)
                wait(act, hBT_full, first + (j - 1 if j else 0))
                act.activation(hB[j % 2][:, :], xr[odd][:, j, 0:D], ACT.Identity, bias=xr[odd][:, j, C_NMR:C_NMR + 1],
                               scale=xr[odd][:, j, C_RSTD:C_RSTD + 1]).then_inc(hB_ready, 1)

            def upper(odd, first, j):
                act.wait_ge(hBT_full, first + (j + 1))
                act.activation(hBT[odd][0][:, j, :, :], tb[:, :].rearrange("p (c k) -> p c k", c=DC),
                               ACT.Copy).then_inc(hBT_hi, 1)

            split1(0, 0, 16)
            n0 = blocks_of(act, 0)
            for j in range(NB):
                def prepare(j):
                    normalise(0, 16, 0, j)
                    upper(0, 0, j)
                per_block(act, n0, j, prepare)
            split2(0, 0, 16)
            with act.Fori(0, NE // 2) as it:
                for odd in range(2):
                    e = it * 2 + odd
                    n, first = blocks_of(act, e), blocks_before(act, e)
                    n_next, first_next = blocks_of(act, e, 1), blocks_before(act, e, 1)
                    row_loads = it * 16 + 16 * (1 + odd)
                    for fq in range(FQ):
                        k0 = first * FQ + n * fq

                        def evacuate(b):
                            act.wait_ge(g1_full, k0 + (b + 1))
                            act.wait_ge(hid_full, k0 + (b - 1 if b else 0))
                            act.activation(g1s[b % 2][:, :], g1p[b % 2], ACT.Copy).then_inc(g1_out, 1)

                        def hidden_upper(b):
                            act.wait_ge(hid_ready, k0 + (b + 1))
                            act.wait_ge(g2_done, k0 + (b - 1 if b else 0))
                            act.activation(hidT[b % 2][0][:, :, :], hid[b % 2][:, :, :], ACT.Relu).then_inc(hidT_hi, 1)

                        with act.If(n_next > fq):
                            normalise(1 - odd, row_loads, first_next, fq)
                        evacuate(0)
                        with act.If(n_next > fq):
                            upper(1 - odd, first_next, fq)
                        u = (fq + 1) % 2
                        loads = it * (16 * FQ) + 16 * ((odd * FQ + fq + 1) // 2 + 1)

                        def next_unit(split, used):
                            def work():
                                act.wait_ge(used, k0)
                                split(u, 0, loads)
                            if odd == 1 and fq == FQ - 1:
                                with act.If(it < NE // 2 - 1):
                                    work()
                            else:
                                work()

                        next_unit(split1, g1_full)

                        def step(b):
                            evacuate(b)
                            hidden_upper(b - 1)

                        per_block(act, n, 1, step)
                        next_unit(split2, g2_done)
                        for b in range(2, NB):
                            per_block(act, n, b, step)
                        for b in range(NB):
                            with act.If(n == b + 1):
                                hidden_upper(b)
                    with act.If(n_next > FQ):
                        normalise(1 - odd, row_loads, first_next, FQ)
                        upper(1 - odd, first_next, FQ)

        @block.vector
        def _(dve):
            done = [0]

            def small(ins):
                ins.then_inc(small_step, 1)
                done[0] += 1
                dve.wait_ge(small_step, done[0])

            small(dve.memset(qmask[:, :], 0.0))
            for hh in range(QH):
                small(dve.memset(qmask[hh * HD:(hh + 1) * HD, hh:hh + 1], 1.0))
            for e in range(NE):
                small(dve.memset(eoff[:, :, e:e + 1], float(e * CAP - 1)))
                small(dve.memset(rank[:, :, e:e + 1], float(NE - e)))
            small(dve.memset(over[:, :, :], DROPPED))
            small(dve.memset(plan_f[:, :], 0.0))
            small(dve.memset(bias[:, :, :], PADDED))
            dve.wait_ge(sides_loaded, 16 * N_SIDES)
            small(dve.copy_predicated(bias[:, :, :], mask_b, fside_b))
            small(dve.tensor_reduce(keys[:, 0, :], mask_b, AX, ALU.add))
            small(dve.reciprocal(keys[:, 1, :], keys[:, 0, :]))
            small(dve.tensor_scalar(keys[:, 0, :], keys[:, 1, :], 0.0, None, ALU.mult))
            for b in range(BATCH):
                small(dve.tensor_scalar(bias[:, b, :], bias[:, b, :], keys[:, 0, b:b + 1], None, ALU.add))
            dve.wait_ge(gates_made, 1)
            dve.tensor_scalar(tgbo[:, :], tgbo[:, :], gt[:, 0:1], None, ALU.mult).then_inc(tgbo_made, 1)

            upper_parts = 0
            for n, (what, w, c) in enumerate(SETUP):
                dve.wait_ge(setup_full, n + 1)
                if what == "wT" and w in (0, 3):
                    upper_parts += 1
                    dve.wait_ge(setup_hi, upper_parts)
                    W = WqT if w == 0 else WoT
                    dve.tensor_tensor(W[1][:, c, :], sbank(n), W[0][:, c, :].bitcast(F32),
                                      ALU.subtract).then_inc(setup_free, 1)
                elif what == "wT":
                    dve.tensor_copy((wkT if w == 1 else wvT)[:, c, :], sbank(n)).then_inc(setup_free, 1)
                elif what == "b1":
                    dve.tensor_copy(b1T[:, :], sbank(n)[:, 0:P]).then_inc(setup_free, 1)
                elif what == "bias":
                    dve.tensor_copy(biasT[:, :], sbank(n)[:, 0:3 * DC]).then_inc(setup_free, 1)
                elif what == "gw":
                    dve.tensor_copy(gwT[:, :, :], sbank(n)[:, 0:DC * NE].rearrange("p (c e) -> p c e", c=DC)).then_inc(setup_free, 1)
                elif what == "cx":
                    dve.tensor_copy(cxT[:, :, w * KEYS:(w + 1) * KEYS],
                                    sbank(n).rearrange("p (c k) -> p c k", c=DC)[:, :, 0:KEYS]).then_inc(setup_free, 1)
                elif what == "k":
                    wait(dve, kb_done, QH * w)
                    dve.tensor_scalar(ktmp[:, :], sbank(n)[:, 0:BATCH * KEYS], bkT[:, w:w + 1], HD ** -0.5,
                                      ALU.add, ALU.mult).then_inc(setup_free, 1)
                    dve.wait_ge(setup_free, n + 1)
                    kt = ktmp[:, :].rearrange("p (b k) -> p b k", b=BATCH)
                    for hh in range(QH):
                        dve.tensor_scalar(KB[0][:, :, w, hh * KEYS:(hh + 1) * KEYS], kt, qmask[:, hh:hh + 1], None,
                                          ALU.mult).then_inc(kb_hi, 1)
                    dve.wait_ge(kb_hi, QH * (w + 1))
                    for hh in range(QH):
                        piece = slice(hh * KEYS, (hh + 1) * KEYS)
                        dve.scalar_tensor_tensor(KB[1][:, :, w, piece], kt, qmask[:, hh:hh + 1],
                                                 KB[0][:, :, w, piece].bitcast(F32), ALU.mult,
                                                 ALU.subtract).then_inc(kb_done, 1)
                elif what == "v":
                    dve.tensor_copy(v_rows[0:KEYS, w, :], sbank(n)[0:KEYS, :]).then_inc(setup_free, 1)
                else:
                    upper_parts += 2
                    dve.wait_ge(setup_hi, upper_parts)
                    for q, (hh, j) in enumerate(VB_PIECES[c]):
                        cols = slice(hh * HD, (hh + 1) * HD)
                        ins = dve.tensor_tensor(VB[1][:, w, :, j, cols],
                                                sbank(n)[:, q * P:(q + 1) * P].rearrange("p (m d) -> p m d", m=DC),
                                                VB[0][:, w, :, j, cols].bitcast(F32), ALU.subtract)
                    ins.then_inc(setup_free, 1)

            def row_stats(g, rows, st, mv, ve, stats, var, scaled):
                for t in range(GT):
                    wait(dve, scaled, g * 3)
                    dve.wait_ge(stats, g * 4 + (t + 1))
                    stand_alone(dve)
                    dve.bn_aggr(mv[:, t, :], st[:, t, :]).then_inc(stats, 1)
                dve.wait_ge(stats, g * 4 + 4)
                dve.tensor_scalar(ve[:, :], mv[:, :, 1], EPS, None, ALU.add).then_inc(var, 1)

            def stats_of_x(g, I2):
                dve.wait_ge(x_loaded[I2[1]], I2[0] * 16 + 16)
                wait(dve, stats1, g * 4)
                for t in range(GT):
                    dve.bn_stats(st1[:, t, :], x_in[I2[1]][:, t, :]).then_inc(stats1, 1)
                row_stats(g, None, st1, mv1, ve1, stats1, var1, scaled1)

            stats_of_x(0, (0, 0))

            def body(I, batch, batch1):
                g, p = num(I), par(I)

                def pt_lower(j):
                    if not has(I, -1):
                        return
                    g1 = num(I, -1)
                    bank, n = ring_use("tp", I, "PT", j)
                    rows = P if j % 3 < 2 else KCH[2]
                    dve.wait_ge(pt_hi, g1 * 6 + (j + 1))
                    dve.tensor_tensor(PT[j // 3][1][0:rows, j % 3, :], tp[bank][0:rows, :],
                                      PT[j // 3][0][0:rows, j % 3, :].bitcast(F32),
                                      ALU.subtract).then_inc(pt_ready, 1)

                def add_bias(t, q):
                    if not has(I, 0):
                        return
                    dve.wait_ge(sc_full[q], g * 2 + (t + 1))
                    half = s[p][:, t, q * 2 * QK:(q + 1) * 2 * QK]
                    dve.tensor_tensor(half.rearrange("p (m h k) -> p m h k", m=2, h=QH),
                                      sc[q][:, :, 0:QK].rearrange("p m (h k) -> p m h k", h=QH),
                                      bias[:, batch, :].unsqueeze(1).unsqueeze(1).to_broadcast([P, 2, QH, KEYS]),
                                      ALU.add).then_inc(s_biased, 1)

                def row_max(t):
                    if not has(I, 0):
                        return
                    dve.wait_ge(s_biased, g * 4 + 2 * t + 2)
                    dve.tensor_reduce(mx[p][:, t, :], s[p][:, t, :].rearrange("p (h k) -> p h k", h=HEADS), AX,
                                      ALU.max).then_inc(max_ready, 1)

                def ctx_lower(q):
                    if not has(I, -1):
                        return
                    g1 = num(I, -1)
                    bank, n = ring_use("acc", I, "AV", q)
                    dve.wait_ge(ctx_hi, g1 * 4 + 2 * (q + 1))
                    for mm in range(2):
                        m = 2 * q + mm
                        dve.scalar_tensor_tensor(ctxT[1][:, m, :], acc[bank][:, mm * GTOK:(mm + 1) * GTOK],
                                                 bvT[:, m:m + 1], ctxT[0][:, m, :].bitcast(F32), ALU.add,
                                                 ALU.subtract).then_inc(ctx_ready, 1)

                def gate():
                    if not has(I, -2):
                        return
                    g2 = num(I, -2)
                    bank, n = ring_use("acc", I, "GATE", 0)
                    k = g2 * GATE_STEPS
                    dve.wait_ge(acc_full[bank], n + 1)
                    wait(dve, gate_step, k)
                    dve.tensor_tensor(lg[:, :, :], acc[bank][:, 0:GT * NE].rearrange("p (t e) -> p t e", t=GT),
                                      gb[:, :].unsqueeze(1).to_broadcast([P, GT, NE]), ALU.add).then_inc(gate_step, 1)
                    dve.wait_ge(gate_step, k + 1)
                    dve.tensor_reduce(lmx[:, :], lg[:, :, :], AX, ALU.max).then_inc(gate_step, 1)
                    dve.wait_ge(gate_step, k + 2)
                    dve.tensor_tensor(lm[:, :, :], lg[:, :, :], lmx[:, :].unsqueeze(2).to_broadcast([P, GT, NE]),
                                      ALU.subtract).then_inc(gate_step, 1)
                    dve.wait_ge(gate_step, k + 3)
                    dve.scalar_tensor_tensor(wr[:, :, :], lm[:, :, :], 0.0, rank[:, :, :], ALU.is_ge,
                                             ALU.mult).then_inc(gate_step, 1)
                    dve.wait_ge(gate_step, k + 4)
                    dve.tensor_reduce(wm[:, :], wr[:, :, :], AX, ALU.max).then_inc(gate_step, 1)
                    dve.wait_ge(gate_step, k + 5)
                    wait(dve, route_step, g2 * ROUTE_STEPS)
                    wait(dve, slot_mixed, g2 * 2)
                    dve.tensor_tensor(oh[:, :, :], wr[:, :, :], wm[:, :].unsqueeze(2).to_broadcast([P, GT, NE]),
                                      ALU.is_equal).then_inc(gate_step, 1)
                def sums(t):
                    if not has(I, 0):
                        return
                    dve.wait_ge(exp_ready, g * 2 + (t + 1))
                    dve.tensor_reduce(den[p][:, t, :], s[p][:, t, :].rearrange("p (h k) -> p h k", h=HEADS), AX,
                                      ALU.add).then_inc(den_ready, 1)
                    dve.wait_ge(den_ready, g * 2 + (t + 1))
                    dve.reciprocal(rden[p][:, t, :], den[p][:, t, :]).then_inc(rden_ready, 1)

                def xnT_lower(j):
                    if not has(I, 1):
                        return
                    bank, n = ring_use("tp", I, "XT", j)
                    dve.wait_ge(xnT_hi, num(I, 1) * 2 + (j + 1))
                    dve.tensor_tensor(xnT[1][:, 2 * j:2 * j + 2, :],
                                      tp[bank][:, :].rearrange("p (c k) -> p c k", c=2),
                                      xnT[0][:, 2 * j:2 * j + 2, :].bitcast(F32),
                                      ALU.subtract).then_inc(xnT_ready, 1)

                def q_lower(q):
                    if not has(I, 1):
                        return
                    bank, n = ring_use("acc", I, "Q", q)
                    dve.wait_ge(q_hi, num(I, 1) * 4 + 2 * (q + 1))
                    for mm in range(2):
                        m = 2 * q + mm
                        dve.scalar_tensor_tensor(qT[1][:, m, :], acc[bank][:, mm * GTOK:(mm + 1) * GTOK],
                                                 bqT[:, m:m + 1], qT[0][:, m, :].bitcast(F32), ALU.add,
                                                 ALU.subtract).then_inc(q_ready, 1)

                def residual(t):
                    if not has(I, -1):
                        return
                    g1, p1 = num(I, -1), par(I, -1)
                    bank, n = ring_use("acc", I, "O", t)
                    dve.wait_ge(acc_full[bank], n + 1)
                    dve.wait_ge(row_based, g1 * 2 + (t + 1))
                    r = row[p1][:, t, 0:D]
                    dve.scalar_tensor_tensor(r, acc[bank][:, :], gt[:, 0:1], r, ALU.mult,
                                             ALU.add).then_inc(x1_ready, 1)
                    dve.wait_ge(x1_ready, g1 * 2 + (t + 1))
                    if t == 0:
                        wait(dve, stats2, g1 * 4)
                    dve.bn_stats(st2[:, t, :], r).then_inc(stats2, 1)

                def cumulative():
                    if not has(I, -2):
                        return
                    g2 = num(I, -2)
                    bank, n = ring_use("acc", I, "CUM", 0)
                    counts = acc[bank][:, 0:GT * NE].rearrange("p (t e) -> p t e", t=GT)
                    dve.wait_ge(acc_full[bank], n + 1)
                    wait(dve, slot_mixed, g2 * 2)
                    dve.scalar_tensor_tensor(cu[:, :, :], counts, float(CAP), over[:, :, :], ALU.is_gt,
                                             ALU.mult).then_inc(cum_read, 1)
                    dve.tensor_tensor(cs[:, :, :], counts, eoff[:, :, :], ALU.add).then_inc(cum_read, 1)
                def slots_of_tokens():
                    if not has(I, -2):
                        return
                    g2 = num(I, -2)
                    dve.wait_ge(gate_exp, g2 + 1)
                    wait(dve, row_ready, g2 * 3)
                    dve.tensor_reduce(exs[:, :], ex[:, :, :], AX, ALU.add).then_inc(top_ready, 1)
                    dve.wait_ge(top_ready, g2 * 2 + 1)
                    dve.reciprocal(exr[:, :], exs[:, :]).then_inc(top_ready, 1)
                    dve.wait_ge(slot_mixed, g2 * 2 + 2)
                    for q in range(2):
                        if is_fixed(I):
                            wait(dve, row_scattered[q], ((g2 + 1 - q) // 2) * 32)
                        else:
                            dve.wait_ge(row_scattered[q], (I[0] - 1 + (1 if I[1] > q else 0)) * 32)
                    with nc.allow_low_precision(reason="sums of small integers, exact in float32 and in int32"):
                        dve.tensor_reduce(slot[:, :], cw[:, :, :], AX, ALU.add).then_inc(slot_ready, 1)

                pt_lower(0)
                add_bias(0, 0)
                pt_lower(1)
                add_bias(0, 1)
                pt_lower(2)
                row_max(0)
                add_bias(1, 0)
                pt_lower(3)
                add_bias(1, 1)
                xnT_lower(0)
                row_max(1)
                ctx_lower(0)
                xnT_lower(1)
                pt_lower(4)
                sums(0)
                pt_lower(5)
                q_lower(0)
                sums(1)
                q_lower(1)
                ctx_lower(1)
                gate()
                residual(0)
                residual(1)
                cumulative()
                if has(I, -1):
                    row_stats(num(I, -1), None, st2, mv2, ve2, stats2, var2, scaled2)
                if has(I, 2):
                    stats_of_x(num(I, 2), (I[0] + 1, I[1]))
                slots_of_tokens()

            attend_bodies(dve, body)

            counts = sc[0][0:1, 0, 0:NE]
            nb = plan_f[:, 0:NE]
            dve.wait_ge(count_ready, 1)
            small(dve.tensor_scalar(nb, counts, float(P), 1.0, ALU.is_gt, ALU.add))
            for j in range(2, NB):
                small(dve.scalar_tensor_tensor(nb, counts, float(P * j), nb, ALU.is_gt, ALU.add))
            small(dve.tensor_tensor_scan(plan_f[:, NE + 2:2 * NE + 2], ones[0:1, 0:NE], nb, 0.0, ALU.mult, ALU.add))
            dve.tensor_copy(plan[:, :], plan_f[:, :]).then_inc(plan_ready, 1)

            dve.wait_ge(phase_b, 1)

            def split1(i, hi):
                dve.wait_ge(w1_hi, hi)
                dve.tensor_tensor(W1[i][1][:, :, :], raw1[i][:, :, :], W1[i][0][:, :, :].bitcast(F32),
                                  ALU.subtract).then_inc(w1_ready, 1)

            def split2(i, hi):
                dve.wait_ge(w2_hi, hi)
                dve.tensor_tensor(W2[i][1][:, :, :], raw2[i][:, :, :], W2[i][0][:, :, :].bitcast(F32),
                                  ALU.subtract).then_inc(w2_ready, 1)

            def lower(odd, first, j):
                dve.wait_ge(hBT_hi, first + (j + 1))
                dve.tensor_tensor(hBT[odd][1][:, j, :, :], tb[:, :].rearrange("p (c k) -> p c k", c=DC),
                                  hBT[odd][0][:, j, :, :].bitcast(F32), ALU.subtract).then_inc(hBT_ready, 1)

            split1(0, 1)
            n0 = blocks_of(dve, 0)
            for j in range(NB):
                per_block(dve, n0, j, lambda j: lower(0, 0, j))
            split2(0, 1)
            with dve.Fori(0, NE // 2) as it:
                for odd in range(2):
                    e = it * 2 + odd
                    n, first = blocks_of(dve, e), blocks_before(dve, e)
                    n_next, first_next = blocks_of(dve, e, 1), blocks_before(dve, e, 1)
                    for fq in range(FQ):
                        k0 = first * FQ + n * fq

                        def hidden(b):
                            dve.wait_ge(hid_full, k0 + (b + 1))
                            dve.tensor_tensor(
                                hid[b % 2][:, :, :], tb[:, :].rearrange("p (c k) -> p c k", c=DC),
                                b1T[:, bass.ds(e * (FF // P) + fq * DC, DC)].unsqueeze(2).to_broadcast([P, DC, P]),
                                ALU.add).then_inc(hid_ready, 1)
                            dve.wait_ge(hidT_hi, k0 + (b + 1))
                            dve.scalar_tensor_tensor(hidT[b % 2][1][:, :, :], hid[b % 2][:, :, :], 0.0,
                                                     hidT[b % 2][0][:, :, :].bitcast(F32), ALU.max,
                                                     ALU.subtract).then_inc(hidT_ready, 1)

                        def result(b):
                            dve.wait_ge(g2_done, k0 + (b + 1))
                            dve.wait_ge(b2_loaded[odd], it * 16 + 16)
                            dve.wait_ge(y_scattered, first * 16 + 16 * (b - 1 if b else 0))
                            dve.tensor_tensor(yo[b % 2][:, :], oacc[b], b2b[odd][:, :], ALU.add).then_inc(y_added, 1)
                            dve.wait_ge(y_added, first + (b + 1))
                            dve.scalar_tensor_tensor(yo[b % 2][:, :], yo[b % 2][:, :], xr[odd][:, b, C_SCALE:C_SCALE + 1],
                                                     xr[odd][:, b, 0:D], ALU.mult, ALU.add).then_inc(y_ready, 1)

                        with dve.If(n_next > fq):
                            lower(1 - odd, first_next, fq)
                        u = (fq + 1) % 2

                        def next_unit(split):
                            if odd == 1 and fq == FQ - 1:
                                with dve.If(it < NE // 2 - 1):
                                    split(u, e * FQ + (fq + 2))
                            else:
                                split(u, e * FQ + (fq + 2))

                        next_unit(split1)

                        def step(b):
                            hidden(b - 1)
                            if fq == FQ - 1 and b >= 2:
                                result(b - 2)

                        per_block(dve, n, 1, step)
                        next_unit(split2)
                        for b in range(2, NB):
                            per_block(dve, n, b, step)
                        for b in range(NB):
                            with dve.If(n == b + 1):
                                hidden(b)
                                if fq == FQ - 1:
                                    if b >= 1:
                                        result(b - 1)
                                    result(b)
                    with dve.If(n_next > FQ):
                        lower(1 - odd, first_next, FQ)

        @block.tensor
        def _(pe):
            pe.wait_ge(consts_made, POOL_CONSTS)
            for n, (what, w, c) in enumerate(SETUP):
                bank = sbank(n)
                wait(pe, setup_free, n - 3)
                if what == "wT":
                    pe.wait_ge(raw_loaded[w], 16)
                    src = (raw_q, raw_k, raw_v, raw_o)[w]
                    for m in range(DC):
                        last = pe.transpose(bank[:, m * P:(m + 1) * P], src[:, m, c * P:(c + 1) * P], ident[:, :])
                elif what == "b1":
                    pe.wait_ge(sides_loaded, 16 * N_SIDES)
                    last = pe.transpose(bank[:, 0:P], b1_rows, ident[:, :])
                elif what == "bias":
                    last = pe.transpose(bank[:, 0:3 * DC], bias_rows, ident[0:3 * DC, 0:3 * DC])
                elif what == "gw":
                    for m in range(DC):
                        last = pe.transpose(bank[:, m * NE:(m + 1) * NE], gw_rows[:, m * P:(m + 1) * P],
                                            ident[0:NE, 0:NE])
                elif what == "cx":
                    pe.wait_ge(ctx_loaded, 16)
                    for m in range(DC):
                        last = pe.transpose(bank[:, m * P:m * P + KEYS], cx_rows[0:KEYS, w, m * P:(m + 1) * P],
                                            ident[0:KEYS, 0:KEYS])
                elif what == "k":
                    pe.wait_ge(setup_free, AT_SETUP[("cx", 1, 0)] + 1)
                    for m in range(DC):
                        last = pe.matmul(bank[:, 0:BATCH * KEYS], wkT[:, m, w * P:(w + 1) * P], cxT[:, m, :],
                                         start=(m == 0), stop=(m == DC - 1))
                elif what == "v":
                    for m in range(DC):
                        last = pe.matmul(bank[0:KEYS, :], cxT[:, m, w * KEYS:(w + 1) * KEYS], wvT[:, m, :],
                                         start=(m == 0), stop=(m == DC - 1))
                else:
                    pe.wait_ge(setup_free, AT_SETUP[("v", 1, 0)] + 1)
                    for q, (hh, j) in enumerate(VB_PIECES[c]):
                        start = P - (hh * KEYS - P * j)
                        heads = v_rows[0:KEYS, w, :].rearrange("p (m h d) -> p m h d", m=DC, h=QH)[:, :, hh, :]
                        last = pe.matmul(bank[:, q * P:(q + 1) * P].rearrange("p (m d) -> p m d", m=DC),
                                         wide[:, start:start + P], heads, start=True, stop=True)
                last.then_inc(setup_full, 1)

            def freed(ring, I, stage, part):
                last = use_before(ring, I, stage, part)
                if last is None:
                    return
                st, pt, g = last
                s_, v_ = {
                    "PT": lambda: (pt_ready, g * 6 + (pt + 1)),
                    "H2T": lambda: (h2T_ready, g * 2 + (pt + 1)),
                    "XT": lambda: (xnT_ready, g * 2 + (pt + 1)),
                    "AV": lambda: (ctx_ready, g * 4 + 2 * (pt + 1)),
                    "GATE": lambda: (gate_step, g * GATE_STEPS + 1),
                    "CUM": lambda: (cum_read, g * 2 + 2),
                    "O": lambda: (x1_ready, g * 2 + (pt + 1)),
                    "Q": lambda: (q_ready, g * 4 + 2 * (pt + 1)),
                }[st]()
                pe.wait_ge(s_, v_)

            def three(out, a, b, cuts_a, cuts_b, first, last):
                pe.matmul(out, cuts_a(a[0]), cuts_b(b[1]), start=first, stop=False, skip_group_check=True)
                pe.matmul(out, cuts_a(a[1]), cuts_b(b[0]), start=False, stop=False, skip_group_check=True)
                return pe.matmul(out, cuts_a(a[0]), cuts_b(b[0]), start=False, stop=last, skip_group_check=True)

            def body(I, batch, batch1):
                g, p = num(I), par(I)

                def probs_t(j):
                    if not has(I, -1):
                        return
                    g1, p1 = num(I, -1), par(I, -1)
                    bank, n = ring_use("tp", I, "PT", j)
                    if j == 0:
                        pe.wait_ge(p_ready, g1 * 2 + 2)
                    freed("tp", I, "PT", j)
                    stand_alone(pe)
                    q, r = j // 3, j % 3
                    for a in range(2):
                        m, chunk = (2 * q + r, a) if r < 2 else (2 * q + a, 2)
                        rows = KCH[chunk]
                        for t in range(GT):
                            col = m * QK + chunk * P
                            last = pe.transpose(tp[bank][0:rows, a * GTOK + t * P:a * GTOK + (t + 1) * P],
                                                s[p1][:, t, col:col + rows], ident[:, :])
                    last.then_inc(tp_full[bank], 1)

                def scores(t, q):
                    if not has(I, 0):
                        return
                    if t == 0 and q == 0:
                        pe.wait_ge(q_ready, g * 4 + 4)
                        if is_fixed(I) and g == 0:
                            pe.wait_ge(kb_done, QH * DC)
                            pe.wait_ge(setup_free, len(SETUP))
                    if is_fixed(I):
                        wait(pe, s_biased, g * 4 + 2 * t + q - 1)
                    else:
                        pe.wait_ge(s_biased, g * 4 + (2 * t + q - 1))
                    for mm in range(2):
                        m = 2 * q + mm
                        last = three(sc[q][:, mm, 0:QK], qT, KB, lambda z: z[:, m, t * P:(t + 1) * P],
                                     lambda z: z[:, batch, m, :], True, True)
                    last.then_inc(sc_full[q], 1)

                def h2_t(j):
                    if not has(I, -2):
                        return
                    pe.wait_ge(h2_ready, num(I, -2) * 2 + 2)
                    bank, n = ring_use("tp", I, "H2T", j)
                    freed("tp", I, "H2T", j)
                    for a in range(2):
                        for t in range(GT):
                            last = pe.transpose(tp[bank][:, a * GTOK + t * P:a * GTOK + (t + 1) * P],
                                                h2[:, t, (2 * j + a) * P:(2 * j + a + 1) * P], ident[:, :])
                    last.then_inc(tp_full[bank], 1)

                def attend(q):
                    if not has(I, -1):
                        return
                    g1 = num(I, -1)
                    bank, n = ring_use("acc", I, "AV", q)
                    freed("acc", I, "AV", q)
                    pe.wait_ge(pt_ready, g1 * 6 + 3 * (q + 1))
                    for mm in range(2):
                        for chunk in range(3):
                            rows = KCH[chunk]
                            part, half = (mm, chunk) if chunk < 2 else (2, mm)
                            last = three(acc[bank][:, mm * GTOK:(mm + 1) * GTOK], VB, PT[q],
                                         lambda z: z[0:rows, batch1, 2 * q + mm, chunk, :],
                                         lambda z: z[0:rows, part, half * GTOK:(half + 1) * GTOK],
                                         chunk == 0, chunk == 2)
                    last.then_inc(acc_full[bank], 1)

                def xn_t(j):
                    if not has(I, 1):
                        return
                    pe.wait_ge(xn_ready, num(I, 1) * 2 + 2)
                    bank, n = ring_use("tp", I, "XT", j)
                    freed("tp", I, "XT", j)
                    for a in range(2):
                        for t in range(GT):
                            last = pe.transpose(tp[bank][:, a * GTOK + t * P:a * GTOK + (t + 1) * P],
                                                x_in[par(I, 1)][:, t, (2 * j + a) * P:(2 * j + a + 1) * P],
                                                ident[:, :])
                    last.then_inc(tp_full[bank], 1)

                def queries(q):
                    if not has(I, 1):
                        return
                    pe.wait_ge(xnT_ready, num(I, 1) * 2 + 2)
                    bank, n = ring_use("acc", I, "Q", q)
                    freed("acc", I, "Q", q)
                    for mm in range(2):
                        for c in range(DC):
                            last = three(acc[bank][:, mm * GTOK:(mm + 1) * GTOK], WqT, xnT,
                                         lambda z: z[:, c, (2 * q + mm) * P:(2 * q + mm + 1) * P],
                                         lambda z: z[:, c, :], c == 0, c == DC - 1)
                    last.then_inc(acc_full[bank], 1)

                def gate_logits():
                    if not has(I, -2):
                        return
                    bank, n = ring_use("acc", I, "GATE", 0)
                    freed("acc", I, "GATE", 0)
                    pe.wait_ge(h2T_ready, num(I, -2) * 2 + 2)
                    for t in range(GT):
                        for c in range(DC):
                            last = pe.matmul(acc[bank][:, t * NE:(t + 1) * NE], h2T[:, c, t * P:(t + 1) * P],
                                             gwT[:, c, :], start=(c == 0), stop=(c == DC - 1))
                    last.then_inc(acc_full[bank], 1)

                def project(t):
                    if not has(I, -1):
                        return
                    bank, n = ring_use("acc", I, "O", t)
                    freed("acc", I, "O", t)
                    pe.wait_ge(ctx_ready, num(I, -1) * 4 + 4)
                    for m in range(DC):
                        last = three(acc[bank][:, :], ctxT, WoT, lambda z: z[:, m, t * P:(t + 1) * P],
                                     lambda z: z[:, m, :], m == 0, m == DC - 1)
                    last.then_inc(acc_full[bank], 1)

                def count_tokens():
                    if not has(I, -2):
                        return
                    bank, n = ring_use("acc", I, "CUM", 0)
                    freed("acc", I, "CUM", 0)
                    if is_fixed(I) and num(I, -2) == 0:
                        pe.wait_ge(consts_made, POOL_CONSTS + 1)
                    pe.wait_ge(route_step, num(I, -2) * ROUTE_STEPS + 3)
                    pe.matmul(acc[bank][:, 0:GT * NE], tri[:, :], oh[:, :, :].rearrange("p t e -> p (t e)"),
                              start=True, stop=False)
                    pe.matmul(acc[bank][:, 0:GT * NE], ones[:, :], pre[:, :, :].rearrange("p t e -> p (t e)"),
                              start=False, stop=True).then_inc(acc_full[bank], 1)

                probs_t(0)
                scores(0, 0)
                probs_t(1)
                scores(0, 1)
                probs_t(2)
                scores(1, 0)
                probs_t(3)
                scores(1, 1)
                xn_t(0)
                attend(0)
                xn_t(1)
                probs_t(4)
                h2_t(0)
                queries(0)
                probs_t(5)
                h2_t(1)
                queries(1)
                attend(1)
                gate_logits()
                project(0)
                project(1)
                count_tokens()

            attend_bodies(pe, body)

            pe.wait_ge(route_step, GROUPS * ROUTE_STEPS)
            pe.matmul(sc[0][:, 0, 0:NE], ones[:, :], run[:, :], start=True, stop=True).then_inc(count_ready, 1)

            pe.wait_ge(phase_b, 1)

            def prepare(first, j, steps):
                pe.wait_ge(hB_ready, first + (j + 1))
                wait(pe, hid_ready, steps)
                wait(pe, hBT_ready, first + j)
                for c in range(DC):
                    last = pe.transpose(tb[:, c * P:(c + 1) * P], hB[j % 2][:, c * P:(c + 1) * P], ident[:, :])
                last.then_inc(hBT_full, 1)

            n0 = blocks_of(pe, 0)
            for j in range(NB):
                per_block(pe, n0, j, lambda j: prepare(0, j, 0))
            with pe.Fori(0, NE // 2) as it:
                for odd in range(2):
                    e = it * 2 + odd
                    n, first = blocks_of(pe, e), blocks_before(pe, e)
                    n_next, first_next = blocks_of(pe, e, 1), blocks_before(pe, e, 1)
                    for fq in range(FQ):
                        k0 = first * FQ + n * fq
                        u = fq % 2

                        def up(b):
                            if fq == 0:
                                pe.wait_ge(hBT_ready, first + (b + 1))
                            pe.wait_ge(g1_out, k0 + (b - 1 if b else 0))
                            for c in range(DC):
                                last = three(g1p[b % 2], hBT[odd], W1[u], lambda z: z[:, b, c, :],
                                             lambda z: z[:, c, :], c == 0, c == DC - 1)
                            last.then_inc(g1_full, 1)

                        def turn(b):
                            pe.wait_ge(g1_out, k0 + (b + 1))
                            pe.wait_ge(hid_ready, k0 + b)
                            if b == 0:
                                if fq == 0:
                                    pe.wait_ge(hBT_ready, first + n)
                                with pe.If(n_next > fq):
                                    pe.wait_ge(hBT_ready, first_next + (fq + 1))
                            for j in range(DC):
                                last = pe.transpose(tb[:, j * P:(j + 1) * P], g1s[b % 2][:, j * P:(j + 1) * P],
                                                    ident[:, :])
                            last.then_inc(hid_full, 1)

                        def down(b):
                            pe.wait_ge(hidT_ready, k0 + (b + 1))
                            if fq == 0:
                                pe.wait_ge(y_added, first)
                            for j in range(DC):
                                last = three(oacc[b], hidT[b % 2], W2[u], lambda z: z[:, j, :],
                                             lambda z: z[:, j, :], fq == 0 and j == 0, fq == FQ - 1 and j == DC - 1)
                            last.then_inc(g2_done, 1)

                        pe.wait_ge(w1_ready, e * FQ + (fq + 1))
                        up(0)
                        with pe.If(n_next > fq):
                            prepare(first_next, fq, k0)

                        def step(b):
                            up(b)
                            turn(b - 1)
                            if b == 2:
                                pe.wait_ge(w2_ready, e * FQ + (fq + 1))
                            if b >= 2:
                                down(b - 2)

                        for b in range(1, NB):
                            per_block(pe, n, b, step)
                        for b in range(NB):
                            with pe.If(n == b + 1):
                                turn(b)
                                if b < 2:
                                    pe.wait_ge(w2_ready, e * FQ + (fq + 1))
                                if b >= 1:
                                    down(b - 1)
                                down(b)
                    with pe.If(n_next > FQ):
                        prepare(first_next, FQ, first_next * FQ)


_INS = ["x", "ctx_1024", "fside_BxS2_0", "mask_BxS2_bk0", "g_xattn", "g_ffn", "L0_xattn_Wq_w", "L0_xattn_Wq_b",
        "L0_xattn_Wkv_w", "L0_xattn_Wkv_b", "L0_xattn_out_w", "L0_xattn_out_b", "L0_ffn_gate_w", "L0_ffn_gate_b",
        "L0_ffn_w1", "L0_ffn_b1", "L0_ffn_w2", "L0_ffn_b2"]


def kernel(**inputs):
    import numpy as _np
    import concourse.bacc as _bacc
    from concourse import mybir as _mybir
    from concourse.bass_utils import run_bass_kernel_spmd as _run

    nc = _bacc.Bacc("TRN2", target_bir_lowering=False, num_devices=1)
    arrays, args = {}, []
    for name in _INS:
        a = _np.ascontiguousarray(inputs[name])
        arrays[f"in_{name}_dram"] = a
        dt = U8 if a.dtype == _np.bool_ else _mybir.dt.from_np(a.dtype)
        args.append(nc.dram_tensor(f"in_{name}_dram", a.shape, dt, kind="ExternalInput").ap())
    out = nc.dram_tensor("out_0_dram", (BATCH, SEQ, D), F32, kind="ExternalOutput").ap()
    flamingo_block(nc, *args, out)
    r = _run(nc, [arrays], core_ids=[0])
    return r.results[0]["out_0_dram"]
```

```python
from contextlib import ExitStack

import concourse.bass as bass
from concourse import mybir

F32 = mybir.dt.float32
F32R = mybir.dt.float32r
I32 = mybir.dt.int32
U8 = mybir.dt.uint8
ALU = mybir.AluOpType
ACT = mybir.ActivationFunctionType
AX = mybir.AxisListType.X

P = 128
BATCH, SEQ, D = 2, 2048, 512
KEYS = 77
HEADS, HD = 16, 32
TOK = BATCH * SEQ
DC = D // P
QH = HEADS // DC
QK = QH * KEYS
KCH = [P, P, QK - 2 * P]
GT = 2
GTOK = GT * P
GROUPS = TOK // GTOK
NE, FF = 8, 2048
CAP = 640
NB = CAP // P
FQ = FF // 512
ROW = D + 4
C_RSTD, C_NMR, C_SCALE, C_TOK = D, D + 1, D + 2, D + 3
EPS = 1e-5
PADDED = -1e30
NO_TOKEN = TOK
LAST_ROWS = 16
DROPPED = 16384.0

TP_USES = [("PT", -1, 0), ("PT", -1, 1), ("PT", -1, 2), ("PT", -1, 3), ("XT", 1, 0), ("XT", 1, 1),
           ("PT", -1, 4), ("H2T", -2, 0), ("PT", -1, 5), ("H2T", -2, 1)]
ACC_USES = [("AV", -1, 0), ("Q", 1, 0), ("Q", 1, 1), ("AV", -1, 1), ("GATE", -2, 0), ("O", -1, 0), ("O", -1, 1),
            ("CUM", -2, 0)]


def number_uses(uses):
    at, n = {}, 0
    for body in range(-1, GROUPS + 2):
        for stage, shift, part in uses:
            if 0 <= body + shift < GROUPS:
                at[(body, stage, part)] = n
                n += 1
    return at


RINGS = {"tp": (number_uses(TP_USES), len(TP_USES)), "acc": (number_uses(ACC_USES), len(ACC_USES))}


def is_fixed(I):
    return isinstance(I[0], int)


def num(I, shift=0):
    return I[0] * 2 + (I[1] + shift)


def par(I, shift=0):
    return (I[1] + shift) % 2


def has(I, shift):
    return not is_fixed(I) or 0 <= num(I, shift) < GROUPS


def ring_use(ring, I, stage, part):
    table, per_body = RINGS[ring]
    if is_fixed(I):
        n = table[(num(I), stage, part)]
        return n % 2, n // 2
    n = table[(2 + I[1], stage, part)]
    return n % 2, (I[0] - 1) * per_body + n // 2


def use_before(ring, I, stage, part):
    table, _ = RINGS[ring]
    body = num(I) if is_fixed(I) else 4 + I[1]
    n = table[(body, stage, part)]
    for (b, st, pt), m in table.items():
        if m == n - 2:
            shift = next(x[1] for x in TP_USES + ACC_USES if x[0] == st)
            return st, pt, num(I, b - body + shift)
    return None


def attend_bodies(eng, body):
    for b in range(-1, 4):
        body((b // 2, b % 2), 0, 0)
    with eng.Fori(2, 4) as h:
        body((h, 0), 0, 0)
        body((h, 1), 0, 0)
    body((4, 0), 1, 0)
    body((4, 1), 1, 1)
    with eng.Fori(5, 7) as h:
        body((h, 0), 1, 1)
        body((h, 1), 1, 1)
    for b in range(14, GROUPS + 2):
        body((b // 2, b % 2), 1, 1)


def wait(eng, sem, value):
    if not isinstance(value, int) or value > 0:
        eng.wait_ge(sem, value)


def beyond(count):
    return count + 1


def begin_at_one(eng, *sems):
    for sem in sems:
        eng.sem_inc(sem, 1)


SETUP = ([("wT", w, c) for w in range(4) for c in range(DC)]
         + [("b1", 0, 0), ("bias", 0, 0), ("gw", 0, 0), ("cx", 0, 0), ("cx", 1, 0)]
         + [("k", m, 0) for m in range(DC)] + [("v", b, 0) for b in range(BATCH)]
         + [("vb", b, r) for b in range(BATCH) for r in range(3)])
AT_SETUP = {use: n for n, use in enumerate(SETUP)}
VB_PIECES = [[(0, 0), (1, 0)], [(1, 1), (2, 1)], [(3, 1), (3, 2)]]
EARLY, LATE = [None, 0, 2, 4], [None, 1, 3, None]
GATE_STEPS, ROUTE_STEPS = 6, 3
POOL_CONSTS = 7
N_SIDES = 10


def flamingo_block(nc, x, ctx_in, fside, mask, g_xattn, g_ffn, wq, bq, wkv, bkv, wo, bo,
                   gate_w, gate_b, w1, b1, w2, b2, out):
    x_rows = x.rearrange("b s d -> (b s) d").rearrange("(t p) d -> p t d", p=P)
    out_flat = out.rearrange("b s d -> (b s) d")
    out_rows = out_flat.rearrange("(t p) d -> p t d", p=P)
    slots = nc.dram_tensor("dispatched_rows", (NE * CAP, ROW), F32, kind="Internal").ap()
    slot_blocks = slots.rearrange("(t p) d -> p t d", p=P)

    es = ExitStack()
    with es:
        def sem(name):
            return es.enter_context(nc.semaphore(name))

        def sb(name, shape, dt=F32, stack=None):
            return (stack or es).enter_context(nc.sbuf_tensor(name, shape, dt))

        ident = sb("ident", [P, P])
        ones_r = sb("ones", [P, P], F32R)
        ones = ones_r[:, :].bitcast(F32)
        tri = sb("tri", [P, P])
        raw1 = [sb(f"raw_w1_{i}", [P, DC, 512]) for i in range(2)]
        raw2 = [sb(f"raw_w2_{i}", [P, DC, 512]) for i in range(2)]
        b1T = sb("b1T", [P, NE * FF // P])
        plan = sb("plan", [1, 32], I32)
        plan_f = sb("plan_f", [1, 32])

        tp = [es.enter_context(nc.psum_tensor(f"tp{i}", [P, 512], F32)) for i in range(2)]
        acc = [es.enter_context(nc.psum_tensor(f"acc{i}", [P, 512], F32)) for i in range(2)]
        sc = [es.enter_context(nc.psum_tensor(f"sc{i}", [P, 2, 512], F32)) for i in range(2)]

        ea = ExitStack()
        A = lambda name, shape, dt=F32: sb(name, shape, dt, ea)
        WqT = [A(f"WqT{i}", [P, DC, D], F32R) for i in "hl"]
        WoT = [A(f"WoT{i}", [P, DC, D], F32R) for i in "hl"]
        KB = [A(f"KB{i}", [P, BATCH, DC, QK], F32R) for i in "hl"]
        VB = [A(f"VB{i}", [P, BATCH, DC, 3, P], F32R) for i in "hl"]
        xnT = [A(f"xnT{i}", [P, DC, GTOK], F32R) for i in "hl"]
        qT = [A(f"qT{i}", [P, DC, GTOK], F32R) for i in "hl"]
        ctxT = [A(f"ctxT{i}", [P, DC, GTOK], F32R) for i in "hl"]
        PT = [[A(f"PT{p}{i}", [P, 3, 512], F32R) for i in "hl"] for p in range(2)]
        s = [A(f"s{i}", [P, GT, HEADS * KEYS]) for i in range(2)]
        x_in = [A(f"x_in{i}", [P, GT, D]) for i in range(2)]
        row = [A(f"row{i}", [P, GT, ROW]) for i in range(2)]
        h2 = A("h2", [P, GT, D])
        h2T = A("h2T", [P, DC, GTOK])
        tgbo = A("tgbo", [P, D])
        bias_parts = A("bias_parts", [2, BATCH, QK], F32R)
        keys = A("keys", [P, 2, BATCH])
        qmask = A("qmask", [P, QH])
        biasT = A("biasT", [P, 3 * DC])
        bqT, bkT, bvT = (biasT[:, i * DC:(i + 1) * DC] for i in range(3))
        gwT = A("gwT", [P, DC, NE])
        gb = A("gb", [P, NE])
        gin = A("gin", [P, 2])
        gt = A("gt", [P, 2])
        eoff = A("eoff", [P, GT, NE])
        rank = A("rank", [P, GT, NE])
        over = A("over", [P, GT, NE])
        mhalf = A("mhalf", [P, GT])
        mx = [A(f"mx{i}", [P, GT, HEADS]) for i in range(2)]
        den = [A(f"den{i}", [P, GT, HEADS]) for i in range(2)]
        rden = [A(f"rden{i}", [P, GT, HEADS]) for i in range(2)]
        st1 = A("st1", [P, GT, 6])
        mv1 = A("mv1", [P, GT, 2])
        ve1 = A("ve1", [P, GT])
        rs1 = A("rs1", [P, GT])
        nm1 = A("nm1", [P, GT])
        nmr1 = A("nmr1", [P, GT])
        st2 = A("st2", [P, GT, 6])
        mv2 = A("mv2", [P, GT, 2])
        ve2 = A("ve2", [P, GT])
        nm2 = A("nm2", [P, GT])
        lg = A("lg", [P, GT, NE])
        lmx = A("lmx", [P, GT])
        lm = A("lm", [P, GT, NE])
        ex = A("ex", [P, GT, NE])
        wr = A("wr", [P, GT, NE])
        wm = A("wm", [P, GT])
        oh = A("oh", [P, GT, NE])
        pre = A("pre", [P, GT, NE])
        run = A("run", [P, NE])
        cs = A("cs", [P, GT, NE])
        cu = A("cu", [P, GT, NE])
        cv = A("cv", [P, GT, NE])
        cw = A("cw", [P, GT, NE])
        slot = A("slot", [P, GT], I32)
        exs = A("exs", [P, GT])
        exr = A("exr", [P, GT])
        tokf = A("tokf", [P, GT])
        s_flat = [buf[:, :, :].rearrange("p t k -> p (t k)") for buf in s]
        wkT, wvT = [flat[:, 0:DC * D].rearrange("p (c n) -> p c n", c=DC) for flat in s_flat]
        cx_rows = h2
        cxT = h2T[:, :, 0:BATCH * KEYS]
        v_rows = h2
        empty = row[0][:, 0, :]
        raw_q, raw_k, raw_v, raw_o = raw1[0], raw1[1], raw2[0], raw2[1]
        wide = s_flat[1][0:KEYS, DC * D:DC * D + 320]
        side_rows = s_flat[0][:, DC * D:DC * D + 2 * P]
        b1_rows, bias_rows = side_rows[:, 0:P], side_rows[0:3 * DC, P:2 * P]
        gw_rows = row[0][0:NE, 1, 0:D]
        bias = row[1][:, 1, 64:64 + BATCH * KEYS].rearrange("p (b k) -> p b k", b=BATCH)
        ktmp = [s_flat[0][:, DC * D + 2 * P:DC * D + 2 * P + BATCH * KEYS],
                row[0][:, 1, 0:BATCH * KEYS]]
        fside_b = row[1][:, 0, 0:BATCH * KEYS].rearrange("p (b k) -> p b k", b=BATCH)
        mask_b = row[1][:, 1, 0:D].bitcast(U8)[:, 0:BATCH * KEYS].rearrange("p (b k) -> p b k", b=BATCH)
        ea.close()

        eb = es.enter_context(ExitStack())
        B = lambda name, shape, dt=F32: sb(name, shape, dt, eb)
        W1 = [[B(f"W1{u}{i}", [P, DC, 512], F32R) for i in "hl"] for u in range(2)]
        W2 = [[B(f"W2{u}{i}", [P, DC, 512], F32R) for i in "hl"] for u in range(2)]
        xr = [B(f"xr{i}", [P, NB, ROW]) for i in range(2)]
        hB = [B(f"hB{i}", [P, D]) for i in range(2)]
        hBT = [[B(f"hBT{p}{i}", [P, NB, DC, P], F32R) for i in "hl"] for p in range(2)]
        g1s = [B(f"g1s{i}", [P, 512]) for i in range(2)]
        hid = [B(f"hid{i}", [P, DC, P]) for i in range(2)]
        hidT = [[B(f"hidT{p}{i}", [P, DC, P], F32R) for i in "hl"] for p in range(2)]
        yo = [B(f"yo{i}", [P, D]) for i in range(2)]
        b2b = [B(f"b2b{i}", [P, D]) for i in range(2)]
        oacc = [acc[0][:, :], acc[1][:, :], sc[0][:, 0, :], sc[0][:, 1, :], sc[1][:, 0, :]]
        g1p = [sc[1][:, 1, :], tp[1][:, :]]
        tb = tp[0]

        waits_passed = sem("waits_passed")
        consts_made = sem("consts_made")
        sides_loaded = sem("sides_loaded")
        raw_loaded = [sem(f"raw_loaded{i}") for i in range(4)]
        ctx_loaded = sem("ctx_loaded")
        empty_made = sem("empty_made")
        slots_cleared = sem("slots_cleared")
        setup_full = sem("setup_full")
        setup_hi = sem("setup_hi")
        setup_free = sem("setup_free")
        gates_made = sem("gates_made")
        small_step = sem("small_step")
        tgbo_made = sem("tgbo_made")
        kb_hi = sem("kb_hi")
        kb_done = sem("kb_done")
        tp_full = [sem(f"tp_full{i}") for i in range(2)]
        acc_full = [sem(f"acc_full{i}") for i in range(2)]
        sc_full = [sem(f"sc_full{i}") for i in range(2)]
        x_loaded = [sem(f"x_loaded{i}") for i in range(2)]
        row_loaded = [sem(f"row_loaded{i}") for i in range(2)]
        stats1 = sem("stats1")
        var1 = sem("var1")
        scaled1 = sem("scaled1")
        xn_ready = sem("xn_ready")
        xnT_hi = sem("xnT_hi")
        xnT_ready = sem("xnT_ready")
        q_hi = sem("q_hi")
        q_ready = sem("q_ready")
        scores_ready = sem("scores_ready")
        max_ready = sem("max_ready")
        s_shifted = sem("s_shifted")
        exp_ready = sem("exp_ready")
        den_ready = sem("den_ready")
        rden_ready = sem("rden_ready")
        p_ready = sem("p_ready")
        pt_hi = sem("pt_hi")
        pt_ready = sem("pt_ready")
        ctx_hi = sem("ctx_hi")
        ctx_ready = sem("ctx_ready")
        phase_b = sem("phase_b")
        row_based = sem("row_based")
        x1_ready = sem("x1_ready")
        stats2 = sem("stats2")
        var2 = sem("var2")
        scaled2 = sem("scaled2")
        h2_ready = sem("h2_ready")
        h2T_ready = sem("h2T_ready")
        gate_step = sem("gate_step")
        gate_exp = sem("gate_exp")
        route_step = sem("route_step")
        cum_read = sem("cum_read")
        slot_mixed = sem("slot_mixed")
        slot_ready = sem("slot_ready")
        top_ready = sem("top_ready")
        row_ready = sem("row_ready")
        row_scattered = [sem(f"row_scattered{i}") for i in range(2)]
        out_stored = [sem(f"out_stored{i}") for i in range(2)]
        plan_ready = sem("plan_ready")
        count_ready = sem("count_ready")
        first_block = sem("first_block")
        xr_loaded = [sem(f"xr_loaded{i}") for i in range(2)]
        b2_loaded = [sem(f"b2_loaded{i}") for i in range(2)]
        w1_loaded = [sem(f"w1_loaded{i}") for i in range(2)]
        w2_loaded = [sem(f"w2_loaded{i}") for i in range(2)]
        w1_hi = sem("w1_hi")
        w2_hi = sem("w2_hi")
        w1_ready = sem("w1_ready")
        w2_ready = sem("w2_ready")
        hB_ready = sem("hB_ready")
        hBT_full = sem("hBT_full")
        hBT_hi = sem("hBT_hi")
        hBT_ready = sem("hBT_ready")
        g1_full = sem("g1_full")
        g1_out = sem("g1_out")
        hid_full = sem("hid_full")
        hid_ready = sem("hid_ready")
        hidT_hi = sem("hidT_hi")
        hidT_ready = sem("hidT_ready")
        g2_done = sem("g2_done")
        y_added = sem("y_added")
        y_ready = sem("y_ready")
        y_scattered = sem("y_scattered")

        def sbank(n):
            return sc[(n // 2) % 2][:, n % 2, :]

        def load_w1(eng, e, fq, i):
            eng.dma_start(raw1[i][:, :, :], w1.rearrange("e (c p) f -> p (e c) f", p=P)[
                :, bass.ds(e * DC, DC), fq * 512:(fq + 1) * 512]).then_inc(w1_loaded[i], 16)

        def load_w2(eng, e, fq, i):
            eng.dma_start(raw2[i][:, :, :], w2.rearrange("e (c p) n -> p (e c) n", p=P)[
                :, bass.ds(e * (FF // P) + fq * DC, DC), :]).then_inc(w2_loaded[i], 16)

        def next_of(e):
            return nc.s_assert_within(e + 1, 1, NE - 1, skip_runtime_bounds_check_because="not for the last expert")

        def load_rows(eng, e, i):
            eng.dma_start(xr[i][:, :, :], slot_blocks[:, bass.ds(e * NB, NB), :]).then_inc(xr_loaded[i], 16)
            eng.dma_start(b2b[i][:, :], b2[bass.ds(e, 1), :].to_broadcast([P, D])).then_inc(b2_loaded[i], 16)

        def blocks_of(eng, e, shift=0):
            return eng.value_load(plan[0:1, bass.ds(e + shift, 1)], min_val=0, max_val=NB)

        def blocks_before(eng, e, shift=0):
            return eng.value_load(plan[0:1, bass.ds(e + (NE + 1 + shift), 1)], min_val=0, max_val=NE * NB)

        def per_block(eng, n, b, work):
            if b == 0:
                work(0)
            else:
                with eng.If(n > b):
                    work(b)

        def unless_last(eng, it, checked, work):
            if checked:
                with eng.If(it < NE // 2 - 1):
                    work()
            else:
                work()

        def stand_alone(eng):
            eng.sem_inc(waits_passed, 1)

        block = es.enter_context(nc.Block())

        @block.sync
        def _(sp):
            sp.dma_start(raw_q[:, :, :], wq.rearrange("(m p) k -> p m k", p=P)).then_inc(raw_loaded[0], 16)
            sp.dma_start(x_in[0][:, :, :], x_rows[:, 0:GT, :]).then_inc(x_loaded[0], 16)
            wkv_v = wkv.rearrange("(m p) k -> p m k", p=P)
            sp.dma_start(raw_k[:, :, :], wkv_v[:, 0:DC, :]).then_inc(raw_loaded[1], 16)
            sp.dma_start(cx_rows[0:KEYS, :, :], ctx_in.rearrange("b s d -> s b d")).then_inc(ctx_loaded, 16)
            sp.dma_start(raw_v[:, :, :], wkv_v[:, DC:2 * DC, :]).then_inc(raw_loaded[2], 16)
            sp.dma_start(raw_o[:, :, :], wo.rearrange("(m p) k -> p m k", p=P)).then_inc(raw_loaded[3], 16)
            sp.dma_start(x_in[1][:, :, :], x_rows[:, GT:2 * GT, :]).then_inc(x_loaded[1], 16)
            sp.wait_ge(empty_made, 2)
            sp.dma_start(slot_blocks, empty.unsqueeze(1).to_broadcast([P, NE * NB, ROW])).then_inc(slots_cleared, 16)
            sp.wait_ge(setup_free, AT_SETUP[("b1", 0, 0)])
            for i in range(2):
                load_w1(sp, 0, i, i)
                load_w2(sp, 0, i, i)

            def body(I, batch, batch1):
                if has(I, -1):
                    before = I[0] + (I[1] - 1) // 2
                    if is_fixed(I) and before == 0:
                        sp.wait_ge(slots_cleared, 16)
                    wait(sp, row_scattered[par(I, -1)], before * 32)
                    stand_alone(sp)
                    wait(sp, out_stored[par(I, -1)], before * 16)
                    stand_alone(sp)
                    sp.dma_start(row[par(I, -1)][:, :, 0:D],
                                 x_rows[:, bass.ds(num(I, -1) * GT, GT), :]).then_inc(row_loaded[par(I, -1)], 16)
                if has(I, 2) and has(I, 0):
                    before = (I[0] + (I[1] - 1) // 2, par(I, -1))
                    bank, n = ring_use("tp", before, "XT", 1)
                    sp.wait_ge(tp_full[bank], n + 1)
                    stand_alone(sp)
                    sp.dma_start(x_in[par(I)][:, :, :],
                                 x_rows[:, bass.ds(num(I, 2) * GT, GT), :]).then_inc(x_loaded[par(I)], 16)
                if has(I, -1):
                    sp.wait_ge(x1_ready, num(I, -1) * 2 + 2)
                    stand_alone(sp)
                    sp.dma_start(out_rows[:, bass.ds(num(I, -1) * GT, GT), :],
                                 row[par(I, -1)][:, :, 0:D]).then_inc(out_stored[par(I, -1)], 16)

            attend_bodies(sp, body)

            for i in range(2):
                sp.wait_ge(out_stored[i], 16 * GROUPS // 2)
                sp.wait_ge(row_scattered[i], 32 * GROUPS // 2 - (LAST_ROWS if i else 0))
            sp.wait_ge(y_scattered, LAST_ROWS)
            sp.wait_ge(plan_ready, 1)
            sp.sem_inc(phase_b, 1)
            sp.dma_start(xr[0][:, 0, :], slot_blocks[:, 0, :]).then_inc(first_block, 16)
            sp.dma_start(xr[0][:, 1:NB, :], slot_blocks[:, 1:NB, :]).then_inc(xr_loaded[0], 16)
            sp.dma_start(b2b[0][:, :], b2[0:1, :].to_broadcast([P, D])).then_inc(b2_loaded[0], 16)
            sp.wait_ge(w1_ready, 1)
            load_w1(sp, 0, 2, 0)
            with sp.Fori(0, NE // 2) as it:
                for odd in range(2):
                    e = it * 2 + odd
                    for fq in range(FQ):
                        def next_w1():
                            sp.wait_ge(w1_ready, e * FQ + (fq + 2))
                            stand_alone(sp)
                            load_w1(sp, e if fq < 1 else next_of(e), (fq + 3) % FQ, (fq + 1) % 2)

                        def next_w2():
                            sp.wait_ge(w2_ready, e * FQ + (fq + 1))
                            stand_alone(sp)
                            load_w2(sp, e if fq < 2 else next_of(e), (fq + 2) % FQ, fq % 2)

                        unless_last(sp, it, odd == 1 and fq >= 1, next_w1)
                        unless_last(sp, it, odd == 1 and fq >= 2, next_w2)
                        if fq == 0:
                            sp.wait_ge(y_scattered, blocks_before(sp, e) * 16 + LAST_ROWS)
                            stand_alone(sp)
                            unless_last(sp, it, odd == 1,
                                        lambda: load_rows(sp, next_of(e) if odd else e + 1, 1 - odd))

        @block.gpsimd
        def _(pool):
            def const(ins):
                ins.then_inc(consts_made, 1)
                const.n += 1
                pool.wait_ge(consts_made, const.n)
            const.n = 0

            const(pool.memset(ident[:, :], 0.0))
            const(pool.affine_select(ident[:, :], ident[:, :], [[-1, P]], ALU.not_equal, 1.0, base=0,
                                     channel_multiplier=1))
            const(pool.memset(ones[:, :], 1.0))
            const(pool.memset(wide[:, :], 0.0))
            const(pool.affine_select(wide[:, :], wide[:, :], [[1, 320]], ALU.not_equal, 1.0, base=-P,
                                     channel_multiplier=-1))
            for part in VB:
                const(pool.memset(part[:, :, :, :, :].bitcast(F32), 0.0))
            assert const.n == POOL_CONSTS
            pool.memset(empty, 0.0).then_inc(empty_made, 1)
            pool.wait_ge(empty_made, 1)
            pool.memset(empty[:, C_TOK:C_TOK + 1].bitcast(I32), NO_TOKEN).then_inc(empty_made, 1)
            const(pool.affine_select(tri[:, :], ones[:, :], [[1, P]], ALU.is_ge, 0.0, base=0,
                                     channel_multiplier=-1))
            const(pool.iota(tokf[:, :], [[P, GT]], base=0, channel_multiplier=1,
                            allow_small_or_imprecise_dtypes=True))
            const(pool.memset(mhalf[:, :], -0.5))
            const(pool.memset(run[:, :], 0.0))

            def norm_scale(g, mv, ve, rstd, nm, nmr, var, scaled):
                pool.wait_ge(var, g + 1)
                pool.tensor_tensor(rstd, ve[:, :], mhalf[:, :], ALU.pow).then_inc(scaled, 1)
                pool.wait_ge(scaled, g * 3 + 1)
                pool.tensor_tensor(nm[:, :], mv[:, :, 0], rstd, ALU.mult).then_inc(scaled, 1)
                pool.wait_ge(scaled, g * 3 + 2)
                stand_alone(pool)
                pool.tensor_scalar(nmr, nm[:, :], -1.0, None, ALU.mult).then_inc(scaled, 1)

            def scale1(g, p):
                wait(pool, xn_ready, g * 2)
                norm_scale(g, mv1, ve1, rs1[:, :], nm1, nmr1[:, :], var1, scaled1)

            scale1(0, 0)

            def body(I, batch, batch1):
                g, p = num(I), par(I)

                def shift(t):
                    if not has(I, 0):
                        return
                    st = s[p][:, t, :].rearrange("p (h k) -> p h k", h=HEADS)
                    pool.wait_ge(max_ready, g * 2 + (t + 1))
                    pool.tensor_tensor(st, st, mx[p][:, t, :].unsqueeze(2).to_broadcast([P, HEADS, KEYS]),
                                       ALU.subtract).then_inc(s_shifted, 1)

                def divide(t):
                    if not has(I, 0):
                        return
                    st = s[p][:, t, :].rearrange("p (h k) -> p h k", h=HEADS)
                    pool.wait_ge(rden_ready, g * 2 + (t + 1))
                    pool.tensor_tensor(st, st, rden[p][:, t, :].unsqueeze(2).to_broadcast([P, HEADS, KEYS]),
                                       ALU.mult).then_inc(p_ready, 1)

                shift(0)
                shift(1)
                divide(0)
                if has(I, 2):
                    scale1(num(I, 2), par(I, 2))
                if has(I, -1):
                    g1, p1 = num(I, -1), par(I, -1)
                    if is_fixed(I) and g1 == 0:
                        pool.wait_ge(tgbo_made, 1)
                    pool.wait_ge(row_loaded[p1], (I[0] + (I[1] - 1) // 2) * 16 + 16)
                    for t in range(GT):
                        r = row[p1][:, t, 0:D]
                        pool.tensor_tensor(r, r, tgbo[:, :], ALU.add).then_inc(row_based, 1)
                if has(I, -2):
                    g2 = num(I, -2)
                    pool.wait_ge(gate_step, g2 * GATE_STEPS + GATE_STEPS)
                    wait(pool, cum_read, g2 * 2)
                    wait(pool, route_step, g2 * ROUTE_STEPS)
                    stand_alone(pool)
                    pool.tensor_copy(pre[:, 0, :], run[:, :]).then_inc(route_step, 1)
                    pool.tensor_tensor(pre[:, 1, :], run[:, :], oh[:, 0, :], ALU.add).then_inc(route_step, 1)
                    pool.wait_ge(route_step, g2 * ROUTE_STEPS + 2)
                    pool.tensor_tensor(run[:, :], pre[:, 1, :], oh[:, 1, :], ALU.add).then_inc(route_step, 1)
                divide(1)
                if has(I, -2):
                    g2, p2 = num(I, -2), par(I, -2)
                    pool.wait_ge(cum_read, g2 * 2 + 2)
                    pool.tensor_tensor(cv[:, :, :], cs[:, :, :], cu[:, :, :], ALU.add).then_inc(slot_mixed, 1)
                    pool.wait_ge(slot_mixed, g2 * 2 + 1)
                    wait(pool, slot_ready, g2)
                    pool.tensor_tensor(cw[:, :, :], cv[:, :, :], oh[:, :, :], ALU.mult).then_inc(slot_mixed, 1)
                if has(I, -1):
                    g1, p1 = num(I, -1), par(I, -1)
                    norm_scale(g1, mv2, ve2, row[p1][:, :, C_RSTD], nm2, row[p1][:, :, C_NMR], var2, scaled2)
                if has(I, -2):
                    pool.wait_ge(top_ready, g2 * 2 + 2)
                    stand_alone(pool)
                    pool.tensor_scalar(row[p2][:, :, C_SCALE], exr[:, :], gt[:, 1:2], None,
                                       ALU.mult).then_inc(row_ready, 1)
                    pool.tensor_copy(row[p2][:, :, C_TOK].bitcast(I32), tokf[:, :]).then_inc(row_ready, 1)
                    pool.wait_ge(row_ready, g2 * 3 + 2)
                    stand_alone(pool)
                    pool.tensor_scalar(tokf[:, :], tokf[:, :], float(GTOK), None, ALU.add).then_inc(row_ready, 1)
                    pool.wait_ge(row_ready, g2 * 3 + 3)
                    pool.wait_ge(slot_ready, g2 + 1)
                    stand_alone(pool)
                    for t in range(GT):
                        very_last = is_fixed(I) and g2 == GROUPS - 1 and t == GT - 1
                        pool.indirect_dma_start(
                            slots, bass.IndirectOffsetOnAxis(ap=slot[:, t:t + 1], axis=0), row[p2][:, t, :], None,
                            bounds_check=NE * CAP - 1, oob_is_err=False).then_inc(
                                y_scattered if very_last else row_scattered[p2], 16)

            attend_bodies(pool, body)

            def split2(i, hi):
                pool.wait_ge(w2_hi, hi)
                stand_alone(pool)
                pool.tensor_tensor(W2[i][1][:, :, :], raw2[i][:, :, :], W2[i][0][:, :, :].bitcast(F32),
                                   ALU.subtract).then_inc(w2_ready, 1)

            split2(0, 1)
            pool.wait_ge(phase_b, 1)
            with pool.Fori(0, NE // 2) as it:
                for odd in range(2):
                    e = it * 2 + odd
                    n, first = blocks_of(pool, e), blocks_before(pool, e)

                    def scatter(b):
                        pool.wait_ge(y_ready, first + (b + 1))
                        stand_alone(pool)
                        pool.wait_ge(y_scattered, first * 16 + b * 16 + LAST_ROWS)
                        stand_alone(pool)
                        pool.indirect_dma_start(
                            out_flat, bass.IndirectOffsetOnAxis(ap=xr[odd][:, b, C_TOK:C_TOK + 1].bitcast(I32), axis=0),
                            yo[b % 2][:, :], None, bounds_check=TOK - 1, oob_is_err=False).then_inc(y_scattered, 16)

                    for fq in range(FQ):
                        unless_last(pool, it, odd == 1 and fq == FQ - 1,
                                    lambda: split2((fq + 1) % 2, e * FQ + (fq + 2)))
                    for b in range(NB):
                        per_block(pool, n, b, scatter)
            pool.wait_ge(y_scattered, blocks_before(pool, 0, NE) * 16 + LAST_ROWS)
            stand_alone(pool)

        @block.scalar
        def _(act):
            begin_at_one(act, g1_out)
            for dst, src in (
                (b1_rows, b1.rearrange("e (c p) -> (e c) p", p=P)),
                (gw_rows, gate_w),
                (bias_rows[0:DC, :], bq.rearrange("(m p) -> m p", p=P)),
                (bias_rows[DC:3 * DC, :], bkv.rearrange("(m p) -> m p", p=P)),
                (gb[:, :], gate_b.unsqueeze(0).to_broadcast([P, NE])),
                (tgbo[:, :], bo.unsqueeze(0).to_broadcast([P, D])),
                (fside_b, fside.unsqueeze(0).to_broadcast([P, BATCH, KEYS])),
                (mask_b, mask.unsqueeze(0).to_broadcast([P, BATCH, KEYS])),
                (gin[:, 0:1], g_xattn.unsqueeze(0).to_broadcast([P, 1])),
                (gin[:, 1:2], g_ffn.unsqueeze(0).to_broadcast([P, 1])),
            ):
                act.dma_start(dst, src).then_inc(sides_loaded, 16)
            def normalise1(g, p):
                act.wait_ge(scaled1, g * 3 + 3)
                for t in range(GT):
                    act.activation(x_in[p][:, t, :], x_in[p][:, t, :], ACT.Identity, bias=nmr1[:, t:t + 1],
                                   scale=rs1[:, t:t + 1]).then_inc(xn_ready, 1)

            for n, (what, w, c) in enumerate(SETUP):
                if what == "wT" and (w, c) == (1, 0):
                    act.wait_ge(sides_loaded, 16 * N_SIDES)
                    act.activation(gt[:, :], gin[:, :], ACT.Tanh).then_inc(gates_made, 1)
                if what == "wT" and w in (0, 3):
                    act.wait_ge(setup_full, n + 1)
                    act.activation((WqT if w == 0 else WoT)[0][:, c, :], sbank(n), ACT.Copy).then_inc(setup_hi, 1)
                elif what == "k":
                    if w == 0:
                        normalise1(0, 0)
                    act.wait_ge(setup_free, n + 1)
                    for hh in range(QH):
                        act.activation(KB[0][:, :, w, hh * KEYS:(hh + 1) * KEYS],
                                       ktmp[w % 2].rearrange("p (b k) -> p b k", b=BATCH), ACT.Identity,
                                       scale=qmask[:, hh:hh + 1]).then_inc(kb_hi, 1)
                elif what == "vb":
                    act.wait_ge(setup_full, n + 1)
                    act.wait_ge(consts_made, POOL_CONSTS)
                    for q, (hh, j) in enumerate(VB_PIECES[c]):
                        act.activation(VB[0][:, w, :, j, hh * HD:(hh + 1) * HD],
                                       sbank(n)[:, q * P:(q + 1) * P].rearrange("p (m d) -> p m d", m=DC),
                                       ACT.Copy).then_inc(setup_hi, 1)

            def body(I, batch, batch1):
                g, p = num(I), par(I)

                def pt_upper(j):
                    if not has(I, -1):
                        return
                    bank, n = ring_use("tp", I, "PT", j)
                    rows = P if j % 3 < 2 else KCH[2]
                    act.wait_ge(tp_full[bank], n + 1)
                    act.activation(PT[j // 3][0][0:rows, j % 3, :], tp[bank][0:rows, :], ACT.Copy).then_inc(pt_hi, 1)

                def scores_out(t, q):
                    if not has(I, 0):
                        return
                    act.wait_ge(sc_full[q], g * 2 + (t + 1))
                    half = s[p][:, t, q * 2 * QK:(q + 1) * 2 * QK]
                    act.activation(half.rearrange("p (m k) -> p m k", m=2), sc[q][:, :, 0:QK],
                                   ACT.Copy).then_inc(scores_ready, 1)

                def exponentials(t):
                    if not has(I, 0):
                        return
                    act.wait_ge(s_shifted, g * 2 + (t + 1))
                    act.activation(s[p][:, t, :], s[p][:, t, :], ACT.Exp).then_inc(exp_ready, 1)

                def xnT_upper(j):
                    if not has(I, 1):
                        return
                    bank, n = ring_use("tp", I, "XT", j)
                    act.wait_ge(tp_full[bank], n + 1)
                    act.activation(xnT[0][:, 2 * j:2 * j + 2, :],
                                   tp[bank][:, :].rearrange("p (c k) -> p c k", c=2), ACT.Copy).then_inc(xnT_hi, 1)

                def h2T_copy(j):
                    if not has(I, -2):
                        return
                    bank, n = ring_use("tp", I, "H2T", j)
                    act.wait_ge(tp_full[bank], n + 1)
                    act.activation(h2T[:, 2 * j:2 * j + 2, :], tp[bank][:, :].rearrange("p (c k) -> p c k", c=2),
                                   ACT.Copy).then_inc(h2T_ready, 1)

                def ctx_upper(q):
                    if not has(I, -1):
                        return
                    bank, n = ring_use("acc", I, "AV", q)
                    act.wait_ge(acc_full[bank], n + 1)
                    for mm in range(2):
                        m = 2 * q + mm
                        act.activation(ctxT[0][:, m, :], acc[bank][:, mm * GTOK:(mm + 1) * GTOK], ACT.Identity,
                                       bias=bvT[:, m:m + 1]).then_inc(ctx_hi, 1)

                def q_upper(q):
                    if not has(I, 1):
                        return
                    bank, n = ring_use("acc", I, "Q", q)
                    act.wait_ge(acc_full[bank], n + 1)
                    for mm in range(2):
                        m = 2 * q + mm
                        act.activation(qT[0][:, m, :], acc[bank][:, mm * GTOK:(mm + 1) * GTOK], ACT.Identity,
                                       bias=bqT[:, m:m + 1]).then_inc(q_hi, 1)

                def normalise2(t):
                    if not has(I, -2):
                        return
                    g2, p2 = num(I, -2), par(I, -2)
                    act.wait_ge(scaled2, g2 * 3 + 3)
                    act.activation(h2[:, t, :], row[p2][:, t, 0:D], ACT.Identity,
                                   bias=row[p2][:, t, C_NMR:C_NMR + 1],
                                   scale=row[p2][:, t, C_RSTD:C_RSTD + 1]).then_inc(h2_ready, 1)

                pt_upper(0)
                scores_out(0, 0)
                pt_upper(1)
                scores_out(0, 1)
                pt_upper(2)
                scores_out(1, 0)
                normalise2(0)
                pt_upper(3)
                scores_out(1, 1)
                xnT_upper(0)
                normalise2(1)
                xnT_upper(1)
                ctx_upper(0)
                exponentials(0)
                pt_upper(4)
                h2T_copy(0)
                pt_upper(5)
                q_upper(0)
                h2T_copy(1)
                exponentials(1)
                q_upper(1)
                ctx_upper(1)
                if has(I, 2):
                    normalise1(num(I, 2), par(I, 2))
                if has(I, -2):
                    act.wait_ge(gate_step, num(I, -2) * GATE_STEPS + 3)
                    act.activation(ex[:, :, :], lm[:, :, :], ACT.Exp).then_inc(gate_exp, 1)

            attend_bodies(act, body)

            def split1(i, loads):
                act.wait_ge(w1_loaded[i], loads)
                act.activation(W1[i][0][:, :, :], raw1[i][:, :, :], ACT.Copy).then_inc(w1_hi, 1)

            def split2(i, loads):
                act.wait_ge(w2_loaded[i], loads)
                act.activation(W2[i][0][:, :, :], raw2[i][:, :, :], ACT.Copy).then_inc(w2_hi, 1)

            def normalise(odd, loads, first, j):
                if loads is None:
                    act.wait_ge(first_block, 16)
                else:
                    act.wait_ge(xr_loaded[odd], loads)
                wait(act, hBT_full, first + (j - 1 if j else 0))
                act.activation(hB[j % 2][:, :], xr[odd][:, j, 0:D], ACT.Identity, bias=xr[odd][:, j, C_NMR:C_NMR + 1],
                               scale=xr[odd][:, j, C_RSTD:C_RSTD + 1]).then_inc(hB_ready, 1)

            def upper(odd, first, j):
                act.wait_ge(hBT_full, first + (j + 1))
                act.activation(hBT[odd][0][:, j, :, :], tb[:, :].rearrange("p (c k) -> p c k", c=DC),
                               ACT.Copy).then_inc(hBT_hi, 1)

            def evacuate(b, count, turned):
                act.wait_ge(g1_full, count)
                act.wait_ge(hid_full, beyond(turned))
                act.activation(g1s[b % 2][:, :], g1p[b % 2], ACT.Copy).then_inc(g1_out, 1)

            split1(0, 16)
            split1(1, 16)
            split2(0, 16)
            act.wait_ge(phase_b, 1)
            n0 = blocks_of(act, 0)
            for j in range(NB):
                def prepare(j):
                    normalise(0, 16 if j else None, 0, j)
                    upper(0, 0, j)
                per_block(act, n0, j, prepare)
            evacuate(0, 1, 0)
            with act.Fori(0, NE // 2) as it:
                for odd in range(2):
                    e = it * 2 + odd
                    n, first = blocks_of(act, e), blocks_before(act, e)
                    n_next, first_next = blocks_of(act, e, 1), first + n
                    row_loads = it * 16 + 16 * (1 + odd)
                    for fq in range(FQ):
                        k0 = first * FQ + n * fq

                        def hidden_upper(b):
                            act.wait_ge(hid_ready, beyond(k0 + (b + 1)))
                            act.wait_ge(g2_done, beyond(k0 + (b - 1 if b else 0)))
                            act.activation(hidT[b % 2][0][:, :, :], hid[b % 2][:, :, :], ACT.Relu).then_inc(hidT_hi, 1)

                        def next_w2():
                            act.wait_ge(g2_done, beyond(k0))
                            split2((fq + 1) % 2, it * (16 * FQ) + 16 * ((odd * FQ + fq + 1) // 2 + 1))

                        def next_w1():
                            act.wait_ge(g1_full, k0 + n)
                            split1(fq % 2, it * (16 * FQ) + 16 * ((odd * FQ + fq + 2) // 2 + 1))

                        def step(b):
                            evacuate(b, k0 + (b + 1), k0 + (b - 1))
                            hidden_upper(b - 1)

                        unless_last(act, it, odd == 1 and fq == FQ - 1, next_w2)
                        if EARLY[fq] is not None:
                            with act.If(n_next > EARLY[fq]):
                                normalise(1 - odd, row_loads, first_next, EARLY[fq])
                        for b in range(1, NB):
                            per_block(act, n, b, step)
                        for b in range(NB):
                            with act.If(n == b + 1):
                                hidden_upper(b)
                        unless_last(act, it, odd == 1 and fq == FQ - 1, lambda: evacuate(0, k0 + (n + 1), k0 + n))
                        if EARLY[fq] is not None:
                            with act.If(n_next > EARLY[fq]):
                                upper(1 - odd, first_next, EARLY[fq])
                        if LATE[fq] is not None:
                            with act.If(n_next > LATE[fq]):
                                normalise(1 - odd, row_loads, first_next, LATE[fq])
                        unless_last(act, it, odd == 1 and fq >= 2, next_w1)
                        if LATE[fq] is not None:
                            with act.If(n_next > LATE[fq]):
                                upper(1 - odd, first_next, LATE[fq])

        @block.vector
        def _(dve):
            begin_at_one(dve, hid_ready, y_added)
            done = [0]

            def small(ins):
                ins.then_inc(small_step, 1)
                done[0] += 1
                dve.wait_ge(small_step, done[0])

            small(dve.memset(qmask[:, :], 0.0))
            for hh in range(QH):
                small(dve.memset(qmask[hh * HD:(hh + 1) * HD, hh:hh + 1], 1.0))
            for e in range(NE):
                small(dve.memset(eoff[:, :, e:e + 1], float(e * CAP - 1)))
                small(dve.memset(rank[:, :, e:e + 1], float(NE - e)))
            small(dve.memset(over[:, :, :], DROPPED))
            small(dve.memset(plan_f[:, :], 0.0))
            small(dve.memset(bias[:, :, :], PADDED))

            def row_stats(g, st, mv, ve, stats, var, scaled):
                for t in range(GT):
                    wait(dve, scaled, g * 3)
                    dve.wait_ge(stats, g * 4 + (t + 1))
                    stand_alone(dve)
                    dve.bn_aggr(mv[:, t, :], st[:, t, :]).then_inc(stats, 1)
                dve.wait_ge(stats, g * 4 + 4)
                dve.tensor_scalar(ve[:, :], mv[:, :, 1], EPS, None, ALU.add).then_inc(var, 1)

            def stats_of_x(g, I2):
                dve.wait_ge(x_loaded[I2[1]], I2[0] * 16 + 16)
                wait(dve, stats1, g * 4)
                for t in range(GT):
                    dve.bn_stats(st1[:, t, :], x_in[I2[1]][:, t, :]).then_inc(stats1, 1)
                row_stats(g, st1, mv1, ve1, stats1, var1, scaled1)

            def keys_lower(m):
                dve.wait_ge(kb_hi, QH * (m + 1))
                kt = ktmp[m % 2].rearrange("p (b k) -> p b k", b=BATCH)
                for hh in range(QH):
                    piece = slice(hh * KEYS, (hh + 1) * KEYS)
                    dve.scalar_tensor_tensor(KB[1][:, :, m, piece], kt, qmask[:, hh:hh + 1],
                                             KB[0][:, :, m, piece].bitcast(F32), ALU.mult,
                                             ALU.subtract).then_inc(kb_done, 1)

            def sides():
                dve.wait_ge(sides_loaded, 16 * N_SIDES)
                small(dve.copy_predicated(bias[:, :, :], mask_b, fside_b))
                small(dve.tensor_reduce(keys[:, 0, :], mask_b, AX, ALU.add))
                small(dve.reciprocal(keys[:, 1, :], keys[:, 0, :]))
                small(dve.tensor_scalar(keys[:, 0, :], keys[:, 1, :], 0.0, None, ALU.mult))
                for b in range(BATCH):
                    small(dve.tensor_scalar(bias[:, b, :], bias[:, b, :], keys[:, 0, b:b + 1], None, ALU.add))
                dve.wait_ge(consts_made, 2)
                low = ktmp[0][0:2, :].rearrange("p (b k) -> p b k", b=BATCH)
                both = bias_parts[:, :, 0:KEYS]
                small(dve.tensor_copy(both, bias[0:2, :, :]))
                small(dve.tensor_tensor(low, bias[0:2, :, :], both.bitcast(F32), ALU.subtract))
                small(dve.tensor_scalar(both, both.bitcast(F32), ident[0:2, 0:1], None, ALU.mult))
                small(dve.scalar_tensor_tensor(both, low, ident[0:2, 1:2], both.bitcast(F32), ALU.mult, ALU.add))
                for hh in range(1, QH):
                    small(dve.tensor_copy(bias_parts[:, :, hh * KEYS:(hh + 1) * KEYS], both.bitcast(F32)))
                dve.wait_ge(gates_made, 1)
                dve.tensor_scalar(tgbo[:, :], tgbo[:, :], gt[:, 0:1], None, ALU.mult).then_inc(tgbo_made, 1)

            stats_of_x(0, (0, 0))
            upper_parts = 0
            for n, (what, w, c) in enumerate(SETUP):
                dve.wait_ge(setup_full, n + 1)
                if what == "wT" and w in (0, 3):
                    upper_parts += 1
                    dve.wait_ge(setup_hi, upper_parts)
                    W = WqT if w == 0 else WoT
                    dve.tensor_tensor(W[1][:, c, :], sbank(n), W[0][:, c, :].bitcast(F32),
                                      ALU.subtract).then_inc(setup_free, 1)
                elif what == "wT":
                    dve.tensor_copy((wkT if w == 1 else wvT)[:, c, :], sbank(n)).then_inc(setup_free, 1)
                elif what == "b1":
                    dve.tensor_copy(b1T[:, :], sbank(n)[:, 0:P]).then_inc(setup_free, 1)
                elif what == "bias":
                    dve.tensor_copy(biasT[:, :], sbank(n)[:, 0:3 * DC]).then_inc(setup_free, 1)
                elif what == "gw":
                    dve.tensor_copy(gwT[:, :, :], sbank(n)[:, 0:DC * NE].rearrange(
                        "p (c e) -> p c e", c=DC)).then_inc(setup_free, 1)
                elif what == "cx":
                    dve.tensor_copy(cxT[:, :, w * KEYS:(w + 1) * KEYS],
                                    sbank(n).rearrange("p (c k) -> p c k", c=DC)[:, :, 0:KEYS]).then_inc(setup_free, 1)
                elif what == "k":
                    wait(dve, kb_done, QH * (w - 1))
                    dve.tensor_scalar(ktmp[w % 2], sbank(n)[:, 0:BATCH * KEYS], bkT[:, w:w + 1], HD ** -0.5,
                                      ALU.add, ALU.mult).then_inc(setup_free, 1)
                    if w:
                        keys_lower(w - 1)
                elif what == "v":
                    if w == 0:
                        keys_lower(DC - 1)
                    dve.tensor_copy(v_rows[0:KEYS, w, :], sbank(n)[0:KEYS, :]).then_inc(setup_free, 1)
                else:
                    upper_parts += 2
                    dve.wait_ge(setup_hi, upper_parts)
                    for q, (hh, j) in enumerate(VB_PIECES[c]):
                        cols = slice(hh * HD, (hh + 1) * HD)
                        ins = dve.tensor_tensor(VB[1][:, w, :, j, cols],
                                                sbank(n)[:, q * P:(q + 1) * P].rearrange("p (m d) -> p m d", m=DC),
                                                VB[0][:, w, :, j, cols].bitcast(F32), ALU.subtract)
                    ins.then_inc(setup_free, 1)

            def body(I, batch, batch1):
                g, p = num(I), par(I)

                def pt_lower(j):
                    if not has(I, -1):
                        return
                    g1 = num(I, -1)
                    bank, n = ring_use("tp", I, "PT", j)
                    rows = P if j % 3 < 2 else KCH[2]
                    dve.wait_ge(pt_hi, g1 * 6 + (j + 1))
                    dve.tensor_tensor(PT[j // 3][1][0:rows, j % 3, :], tp[bank][0:rows, :],
                                      PT[j // 3][0][0:rows, j % 3, :].bitcast(F32),
                                      ALU.subtract).then_inc(pt_ready, 1)

                def row_max(t):
                    if not has(I, 0):
                        return
                    dve.wait_ge(scores_ready, g * 4 + 2 * t + 2)
                    dve.tensor_reduce(mx[p][:, t, :], s[p][:, t, :].rearrange("p (h k) -> p h k", h=HEADS), AX,
                                      ALU.max).then_inc(max_ready, 1)

                def ctx_lower(q):
                    if not has(I, -1):
                        return
                    g1 = num(I, -1)
                    bank, n = ring_use("acc", I, "AV", q)
                    dve.wait_ge(ctx_hi, g1 * 4 + 2 * (q + 1))
                    for mm in range(2):
                        m = 2 * q + mm
                        dve.scalar_tensor_tensor(ctxT[1][:, m, :], acc[bank][:, mm * GTOK:(mm + 1) * GTOK],
                                                 bvT[:, m:m + 1], ctxT[0][:, m, :].bitcast(F32), ALU.add,
                                                 ALU.subtract).then_inc(ctx_ready, 1)

                def gate():
                    if not has(I, -2):
                        return
                    g2 = num(I, -2)
                    bank, n = ring_use("acc", I, "GATE", 0)
                    k = g2 * GATE_STEPS
                    dve.wait_ge(acc_full[bank], n + 1)
                    wait(dve, gate_step, k)
                    dve.tensor_tensor(lg[:, :, :], acc[bank][:, 0:GT * NE].rearrange("p (t e) -> p t e", t=GT),
                                      gb[:, :].unsqueeze(1).to_broadcast([P, GT, NE]), ALU.add).then_inc(gate_step, 1)
                    dve.wait_ge(gate_step, k + 1)
                    dve.tensor_reduce(lmx[:, :], lg[:, :, :], AX, ALU.max).then_inc(gate_step, 1)
                    dve.wait_ge(gate_step, k + 2)
                    dve.tensor_tensor(lm[:, :, :], lg[:, :, :], lmx[:, :].unsqueeze(2).to_broadcast([P, GT, NE]),
                                      ALU.subtract).then_inc(gate_step, 1)
                    dve.wait_ge(gate_step, k + 3)
                    dve.scalar_tensor_tensor(wr[:, :, :], lm[:, :, :], 0.0, rank[:, :, :], ALU.is_ge,
                                             ALU.mult).then_inc(gate_step, 1)
                    dve.wait_ge(gate_step, k + 4)
                    dve.tensor_reduce(wm[:, :], wr[:, :, :], AX, ALU.max).then_inc(gate_step, 1)
                    dve.wait_ge(gate_step, k + 5)
                    wait(dve, route_step, g2 * ROUTE_STEPS)
                    wait(dve, slot_mixed, g2 * 2)
                    dve.tensor_tensor(oh[:, :, :], wr[:, :, :], wm[:, :].unsqueeze(2).to_broadcast([P, GT, NE]),
                                      ALU.is_equal).then_inc(gate_step, 1)

                def sums(t):
                    if not has(I, 0):
                        return
                    dve.wait_ge(exp_ready, g * 2 + (t + 1))
                    dve.tensor_reduce(den[p][:, t, :], s[p][:, t, :].rearrange("p (h k) -> p h k", h=HEADS), AX,
                                      ALU.add).then_inc(den_ready, 1)
                    dve.wait_ge(den_ready, g * 2 + (t + 1))
                    dve.reciprocal(rden[p][:, t, :], den[p][:, t, :]).then_inc(rden_ready, 1)

                def xnT_lower(j):
                    if not has(I, 1):
                        return
                    bank, n = ring_use("tp", I, "XT", j)
                    dve.wait_ge(xnT_hi, num(I, 1) * 2 + (j + 1))
                    dve.tensor_tensor(xnT[1][:, 2 * j:2 * j + 2, :],
                                      tp[bank][:, :].rearrange("p (c k) -> p c k", c=2),
                                      xnT[0][:, 2 * j:2 * j + 2, :].bitcast(F32),
                                      ALU.subtract).then_inc(xnT_ready, 1)

                def q_lower(q):
                    if not has(I, 1):
                        return
                    bank, n = ring_use("acc", I, "Q", q)
                    dve.wait_ge(q_hi, num(I, 1) * 4 + 2 * (q + 1))
                    for mm in range(2):
                        m = 2 * q + mm
                        dve.scalar_tensor_tensor(qT[1][:, m, :], acc[bank][:, mm * GTOK:(mm + 1) * GTOK],
                                                 bqT[:, m:m + 1], qT[0][:, m, :].bitcast(F32), ALU.add,
                                                 ALU.subtract).then_inc(q_ready, 1)

                def residual(t):
                    if not has(I, -1):
                        return
                    g1, p1 = num(I, -1), par(I, -1)
                    bank, n = ring_use("acc", I, "O", t)
                    dve.wait_ge(acc_full[bank], n + 1)
                    dve.wait_ge(row_based, g1 * 2 + (t + 1))
                    r = row[p1][:, t, 0:D]
                    dve.scalar_tensor_tensor(r, acc[bank][:, :], gt[:, 0:1], r, ALU.mult,
                                             ALU.add).then_inc(x1_ready, 1)
                    dve.wait_ge(x1_ready, g1 * 2 + (t + 1))
                    if t == 0:
                        wait(dve, stats2, g1 * 4)
                    dve.bn_stats(st2[:, t, :], r).then_inc(stats2, 1)

                def cumulative():
                    if not has(I, -2):
                        return
                    g2 = num(I, -2)
                    bank, n = ring_use("acc", I, "CUM", 0)
                    counts = acc[bank][:, 0:GT * NE].rearrange("p (t e) -> p t e", t=GT)
                    dve.wait_ge(acc_full[bank], n + 1)
                    wait(dve, slot_mixed, g2 * 2)
                    dve.scalar_tensor_tensor(cu[:, :, :], counts, float(CAP), over[:, :, :], ALU.is_gt,
                                             ALU.mult).then_inc(cum_read, 1)
                    dve.tensor_tensor(cs[:, :, :], counts, eoff[:, :, :], ALU.add).then_inc(cum_read, 1)

                def slots_of_tokens():
                    if not has(I, -2):
                        return
                    g2 = num(I, -2)
                    dve.wait_ge(gate_exp, g2 + 1)
                    wait(dve, row_ready, g2 * 3)
                    dve.tensor_reduce(exs[:, :], ex[:, :, :], AX, ALU.add).then_inc(top_ready, 1)
                    dve.wait_ge(top_ready, g2 * 2 + 1)
                    dve.reciprocal(exr[:, :], exs[:, :]).then_inc(top_ready, 1)
                    dve.wait_ge(slot_mixed, g2 * 2 + 2)
                    for q in range(2):
                        if is_fixed(I):
                            wait(dve, row_scattered[q], ((g2 + 1 - q) // 2) * 32)
                        else:
                            dve.wait_ge(row_scattered[q], (I[0] - 1 + (1 if I[1] > q else 0)) * 32)
                    with nc.allow_low_precision(reason="sums of small integers, exact in float32 and in int32"):
                        dve.tensor_reduce(slot[:, :], cw[:, :, :], AX, ALU.add).then_inc(slot_ready, 1)

                pt_lower(0)
                pt_lower(1)
                pt_lower(2)
                row_max(0)
                pt_lower(3)
                xnT_lower(0)
                xnT_lower(1)
                if not has(I, 0) and num(I) < 0:
                    sides()
                row_max(1)
                ctx_lower(0)
                pt_lower(4)
                sums(0)
                pt_lower(5)
                q_lower(0)
                if has(I, 2):
                    stats_of_x(num(I, 2), (I[0] + 1, I[1]))
                q_lower(1)
                ctx_lower(1)
                gate()
                sums(1)
                residual(0)
                residual(1)
                cumulative()
                if has(I, -1):
                    row_stats(num(I, -1), st2, mv2, ve2, stats2, var2, scaled2)
                slots_of_tokens()

            attend_bodies(dve, body)

            counts = sc[0][0:1, 0, 0:NE]
            nb = plan_f[:, 0:NE]
            dve.wait_ge(count_ready, 1)
            small(dve.tensor_scalar(nb, counts, float(P), 1.0, ALU.is_gt, ALU.add))
            for j in range(2, NB):
                small(dve.scalar_tensor_tensor(nb, counts, float(P * j), nb, ALU.is_gt, ALU.add))
            small(dve.tensor_tensor_scan(plan_f[:, NE + 2:2 * NE + 2], ones[0:1, 0:NE], nb, 0.0, ALU.mult, ALU.add))
            dve.tensor_copy(plan[:, :], plan_f[:, :]).then_inc(plan_ready, 1)

            def split1(i, hi):
                dve.wait_ge(w1_hi, hi)
                dve.tensor_tensor(W1[i][1][:, :, :], raw1[i][:, :, :], W1[i][0][:, :, :].bitcast(F32),
                                  ALU.subtract).then_inc(w1_ready, 1)

            def lower(odd, first, j):
                dve.wait_ge(hBT_hi, first + (j + 1))
                dve.tensor_tensor(hBT[odd][1][:, j, :, :], tb[:, :].rearrange("p (c k) -> p c k", c=DC),
                                  hBT[odd][0][:, j, :, :].bitcast(F32), ALU.subtract).then_inc(hBT_ready, 1)

            split1(0, 1)
            split1(1, 2)
            dve.wait_ge(phase_b, 1)
            n0 = blocks_of(dve, 0)
            for j in range(NB):
                per_block(dve, n0, j, lambda j: lower(0, 0, j))
            with dve.Fori(0, NE // 2) as it:
                for odd in range(2):
                    e = it * 2 + odd
                    n, first = blocks_of(dve, e), blocks_before(dve, e)
                    n_next, first_next = blocks_of(dve, e, 1), first + n
                    for fq in range(FQ):
                        k0 = first * FQ + n * fq

                        def hidden(b):
                            dve.wait_ge(hid_full, beyond(k0 + (b + 1)))
                            dve.tensor_tensor(
                                hid[b % 2][:, :, :], tb[:, :].rearrange("p (c k) -> p c k", c=DC),
                                b1T[:, bass.ds(e * (FF // P) + fq * DC, DC)].unsqueeze(2).to_broadcast([P, DC, P]),
                                ALU.add).then_inc(hid_ready, 1)
                            dve.wait_ge(hidT_hi, k0 + (b + 1))
                            dve.scalar_tensor_tensor(hidT[b % 2][1][:, :, :], hid[b % 2][:, :, :], 0.0,
                                                     hidT[b % 2][0][:, :, :].bitcast(F32), ALU.max,
                                                     ALU.subtract).then_inc(hidT_ready, 1)

                        def result(b):
                            dve.wait_ge(g2_done, beyond(k0 + (b + 1)))
                            dve.wait_ge(b2_loaded[odd], it * 16 + 16)
                            dve.wait_ge(y_scattered, first * 16 + 16 * (b - 1 if b else 0) + LAST_ROWS)
                            dve.tensor_tensor(yo[b % 2][:, :], oacc[b], b2b[odd][:, :], ALU.add).then_inc(y_added, 1)
                            dve.wait_ge(y_added, beyond(first + (b + 1)))
                            dve.scalar_tensor_tensor(yo[b % 2][:, :], yo[b % 2][:, :], xr[odd][:, b, C_SCALE:C_SCALE + 1],
                                                     xr[odd][:, b, 0:D], ALU.mult, ALU.add).then_inc(y_ready, 1)

                        def step(b):
                            hidden(b - 1)
                            if fq == FQ - 1 and b >= 2:
                                result(b - 2)

                        for b in range(1, NB):
                            per_block(dve, n, b, step)
                        for b in range(NB):
                            with dve.If(n == b + 1):
                                hidden(b)
                        if EARLY[fq] is not None:
                            with dve.If(n_next > EARLY[fq]):
                                lower(1 - odd, first_next, EARLY[fq])
                        if fq == FQ - 1:
                            for b in range(NB):
                                with dve.If(n == b + 1):
                                    if b >= 1:
                                        result(b - 1)
                                    result(b)
                        unless_last(dve, it, odd == 1 and fq >= 2, lambda: split1(fq % 2, e * FQ + (fq + 3)))
                        if LATE[fq] is not None:
                            with dve.If(n_next > LATE[fq]):
                                lower(1 - odd, first_next, LATE[fq])

        @block.tensor
        def _(pe):
            begin_at_one(pe, hid_full, g2_done)
            pe.wait_ge(consts_made, 2)
            for n, (what, w, c) in enumerate(SETUP):
                bank = sbank(n)
                wait(pe, setup_free, n - 3)
                if what == "wT":
                    pe.wait_ge(raw_loaded[w], 16)
                    src = (raw_q, raw_k, raw_v, raw_o)[w]
                    for m in range(DC):
                        last = pe.transpose(bank[:, m * P:(m + 1) * P], src[:, m, c * P:(c + 1) * P], ident[:, :])
                elif what == "b1":
                    pe.wait_ge(sides_loaded, 16 * N_SIDES)
                    last = pe.transpose(bank[:, 0:P], b1_rows, ident[:, :])
                elif what == "bias":
                    last = pe.transpose(bank[:, 0:3 * DC], bias_rows, ident[0:3 * DC, 0:3 * DC])
                elif what == "gw":
                    for m in range(DC):
                        last = pe.transpose(bank[:, m * NE:(m + 1) * NE], gw_rows[:, m * P:(m + 1) * P],
                                            ident[0:NE, 0:NE])
                elif what == "cx":
                    pe.wait_ge(ctx_loaded, 16)
                    for m in range(DC):
                        last = pe.transpose(bank[:, m * P:m * P + KEYS], cx_rows[0:KEYS, w, m * P:(m + 1) * P],
                                            ident[0:KEYS, 0:KEYS])
                elif what == "k":
                    pe.wait_ge(setup_free, AT_SETUP[("cx", 1, 0)] + 1)
                    for m in range(DC):
                        last = pe.matmul(bank[:, 0:BATCH * KEYS], wkT[:, m, w * P:(w + 1) * P], cxT[:, m, :],
                                         start=(m == 0), stop=(m == DC - 1))
                elif what == "v":
                    for m in range(DC):
                        last = pe.matmul(bank[0:KEYS, :], cxT[:, m, w * KEYS:(w + 1) * KEYS], wvT[:, m, :],
                                         start=(m == 0), stop=(m == DC - 1))
                else:
                    pe.wait_ge(consts_made, POOL_CONSTS)
                    pe.wait_ge(setup_free, AT_SETUP[("v", 1, 0)] + 1)
                    for q, (hh, j) in enumerate(VB_PIECES[c]):
                        start = P - (hh * KEYS - P * j)
                        heads = v_rows[0:KEYS, w, :].rearrange("p (m h d) -> p m h d", m=DC, h=QH)[:, :, hh, :]
                        last = pe.matmul(bank[:, q * P:(q + 1) * P].rearrange("p (m d) -> p m d", m=DC),
                                         wide[:, start:start + P], heads, start=True, stop=True)
                last.then_inc(setup_full, 1)

            def freed(ring, I, stage, part):
                last = use_before(ring, I, stage, part)
                if last is None:
                    return
                st, pt, g = last
                s_, v_ = {
                    "PT": lambda: (pt_ready, g * 6 + (pt + 1)),
                    "H2T": lambda: (h2T_ready, g * 2 + (pt + 1)),
                    "XT": lambda: (xnT_ready, g * 2 + (pt + 1)),
                    "AV": lambda: (ctx_ready, g * 4 + 2 * (pt + 1)),
                    "GATE": lambda: (gate_step, g * GATE_STEPS + 1),
                    "CUM": lambda: (cum_read, g * 2 + 2),
                    "O": lambda: (x1_ready, g * 2 + (pt + 1)),
                    "Q": lambda: (q_ready, g * 4 + 2 * (pt + 1)),
                }[st]()
                pe.wait_ge(s_, v_)

            def three(out, a, b, cuts_a, cuts_b, first, last):
                pe.matmul(out, cuts_a(a[0]), cuts_b(b[1]), start=first, stop=False, skip_group_check=True)
                pe.matmul(out, cuts_a(a[1]), cuts_b(b[0]), start=False, stop=False, skip_group_check=True)
                return pe.matmul(out, cuts_a(a[0]), cuts_b(b[0]), start=False, stop=last, skip_group_check=True)

            def body(I, batch, batch1):
                g = num(I)

                def probs_t(j):
                    if not has(I, -1):
                        return
                    g1, p1 = num(I, -1), par(I, -1)
                    bank, n = ring_use("tp", I, "PT", j)
                    if j == 0:
                        pe.wait_ge(p_ready, g1 * 2 + 2)
                    freed("tp", I, "PT", j)
                    stand_alone(pe)
                    q, r = j // 3, j % 3
                    for a in range(2):
                        m, chunk = (2 * q + r, a) if r < 2 else (2 * q + a, 2)
                        rows = KCH[chunk]
                        for t in range(GT):
                            col = m * QK + chunk * P
                            last = pe.transpose(tp[bank][0:rows, a * GTOK + t * P:a * GTOK + (t + 1) * P],
                                                s[p1][:, t, col:col + rows], ident[:, :])
                    last.then_inc(tp_full[bank], 1)

                def scores(t, q):
                    if not has(I, 0):
                        return
                    if t == 0 and q == 0:
                        pe.wait_ge(q_ready, g * 4 + 4)
                        if is_fixed(I) and g == 0:
                            pe.wait_ge(kb_done, QH * DC)
                            pe.wait_ge(tgbo_made, 1)
                            pe.wait_ge(setup_free, len(SETUP))
                    if is_fixed(I):
                        wait(pe, scores_ready, g * 4 + 2 * t + q - 1)
                    else:
                        pe.wait_ge(scores_ready, g * 4 + (2 * t + q - 1))
                    for mm in range(2):
                        m = 2 * q + mm
                        pe.matmul(sc[q][:, mm, 0:QK], ones_r[0:2, :], bias_parts[:, batch, :],
                                  start=True, stop=False, skip_group_check=True)
                        last = three(sc[q][:, mm, 0:QK], qT, KB, lambda z: z[:, m, t * P:(t + 1) * P],
                                     lambda z: z[:, batch, m, :], False, True)
                    last.then_inc(sc_full[q], 1)

                def h2_t(j):
                    if not has(I, -2):
                        return
                    pe.wait_ge(h2_ready, num(I, -2) * 2 + 2)
                    bank, n = ring_use("tp", I, "H2T", j)
                    freed("tp", I, "H2T", j)
                    for a in range(2):
                        for t in range(GT):
                            last = pe.transpose(tp[bank][:, a * GTOK + t * P:a * GTOK + (t + 1) * P],
                                                h2[:, t, (2 * j + a) * P:(2 * j + a + 1) * P], ident[:, :])
                    last.then_inc(tp_full[bank], 1)

                def attend(q):
                    if not has(I, -1):
                        if q == 0:
                            xn_t(1)
                        return
                    g1 = num(I, -1)
                    bank, n = ring_use("acc", I, "AV", q)
                    freed("acc", I, "AV", q)
                    pe.wait_ge(pt_ready, g1 * 6 + 3 * (q + 1))
                    for mm in range(2):
                        for chunk in range(3):
                            rows = KCH[chunk]
                            part, half = (mm, chunk) if chunk < 2 else (2, mm)
                            last = three(acc[bank][:, mm * GTOK:(mm + 1) * GTOK], VB, PT[q],
                                         lambda z: z[0:rows, batch1, 2 * q + mm, chunk, :],
                                         lambda z: z[0:rows, part, half * GTOK:(half + 1) * GTOK],
                                         chunk == 0, chunk == 2)
                        if q == 0 and mm == 0:
                            xn_t(1)
                    last.then_inc(acc_full[bank], 1)

                def xn_t(j):
                    if not has(I, 1):
                        return
                    pe.wait_ge(xn_ready, num(I, 1) * 2 + 2)
                    bank, n = ring_use("tp", I, "XT", j)
                    freed("tp", I, "XT", j)
                    for a in range(2):
                        for t in range(GT):
                            last = pe.transpose(tp[bank][:, a * GTOK + t * P:a * GTOK + (t + 1) * P],
                                                x_in[par(I, 1)][:, t, (2 * j + a) * P:(2 * j + a + 1) * P],
                                                ident[:, :])
                    last.then_inc(tp_full[bank], 1)

                def queries(q):
                    if not has(I, 1):
                        return
                    pe.wait_ge(xnT_ready, num(I, 1) * 2 + 2)
                    bank, n = ring_use("acc", I, "Q", q)
                    freed("acc", I, "Q", q)
                    for mm in range(2):
                        for c in range(DC):
                            last = three(acc[bank][:, mm * GTOK:(mm + 1) * GTOK], WqT, xnT,
                                         lambda z: z[:, c, (2 * q + mm) * P:(2 * q + mm + 1) * P],
                                         lambda z: z[:, c, :], c == 0, c == DC - 1)
                    last.then_inc(acc_full[bank], 1)

                def gate_logits():
                    if not has(I, -2):
                        return
                    bank, n = ring_use("acc", I, "GATE", 0)
                    freed("acc", I, "GATE", 0)
                    pe.wait_ge(h2T_ready, num(I, -2) * 2 + 2)
                    for t in range(GT):
                        for c in range(DC):
                            last = pe.matmul(acc[bank][:, t * NE:(t + 1) * NE], h2T[:, c, t * P:(t + 1) * P],
                                             gwT[:, c, :], start=(c == 0), stop=(c == DC - 1))
                    last.then_inc(acc_full[bank], 1)

                def project(t):
                    if not has(I, -1):
                        return
                    bank, n = ring_use("acc", I, "O", t)
                    freed("acc", I, "O", t)
                    pe.wait_ge(ctx_ready, num(I, -1) * 4 + 4)
                    for m in range(DC):
                        last = three(acc[bank][:, :], ctxT, WoT, lambda z: z[:, m, t * P:(t + 1) * P],
                                     lambda z: z[:, m, :], m == 0, m == DC - 1)
                    last.then_inc(acc_full[bank], 1)

                def count_tokens():
                    if not has(I, -2):
                        return
                    bank, n = ring_use("acc", I, "CUM", 0)
                    freed("acc", I, "CUM", 0)
                    if is_fixed(I) and num(I, -2) == 0:
                        pe.wait_ge(consts_made, POOL_CONSTS + 1)
                    pe.wait_ge(route_step, num(I, -2) * ROUTE_STEPS + 3)
                    pe.matmul(acc[bank][:, 0:GT * NE], tri[:, :], oh[:, :, :].rearrange("p t e -> p (t e)"),
                              start=True, stop=False)
                    pe.matmul(acc[bank][:, 0:GT * NE], ones[:, :], pre[:, :, :].rearrange("p t e -> p (t e)"),
                              start=False, stop=True).then_inc(acc_full[bank], 1)

                probs_t(0)
                scores(0, 0)
                probs_t(1)
                scores(0, 1)
                probs_t(2)
                scores(1, 0)
                probs_t(3)
                scores(1, 1)
                xn_t(0)
                attend(0)
                probs_t(4)
                h2_t(0)
                queries(0)
                probs_t(5)
                h2_t(1)
                queries(1)
                attend(1)
                gate_logits()
                project(0)
                project(1)
                count_tokens()

            attend_bodies(pe, body)

            pe.wait_ge(route_step, GROUPS * ROUTE_STEPS)
            pe.matmul(sc[0][:, 0, 0:NE], ones[:, :], run[:, :], start=True, stop=True).then_inc(count_ready, 1)

            pe.wait_ge(phase_b, 1)

            def prepare(first, j, steps):
                pe.wait_ge(hB_ready, first + (j + 1))
                pe.wait_ge(hid_ready, beyond(steps))
                wait(pe, hBT_ready, first + j)
                for c in range(DC):
                    last = pe.transpose(tb[:, c * P:(c + 1) * P], hB[j % 2][:, c * P:(c + 1) * P], ident[:, :])
                last.then_inc(hBT_full, 1)

            def up(odd, u, b, chunks):
                for c in chunks:
                    last = three(g1p[b % 2], hBT[odd], W1[u], lambda z: z[:, b, c, :],
                                 lambda z: z[:, c, :], c == 0, c == DC - 1)
                if c == DC - 1:
                    last.then_inc(g1_full, 1)

            n0 = blocks_of(pe, 0)
            prepare(0, 0, 0)
            pe.wait_ge(w1_ready, 1)
            pe.wait_ge(hBT_ready, 1)
            up(0, 0, 0, range(DC))
            for j in range(1, NB):
                per_block(pe, n0, j, lambda j: prepare(0, j, 0))
            with pe.Fori(0, NE // 2) as it:
                for odd in range(2):
                    e = it * 2 + odd
                    n, first = blocks_of(pe, e), blocks_before(pe, e)
                    n_next, first_next = blocks_of(pe, e, 1), first + n
                    for fq in range(FQ):
                        k0 = first * FQ + n * fq
                        u = fq % 2

                        def turn(b):
                            pe.wait_ge(g1_out, beyond(k0 + (b + 1)))
                            pe.wait_ge(hid_ready, beyond(k0 + b))
                            if b == 0:
                                if fq == 0:
                                    pe.wait_ge(hBT_ready, first + n)
                                else:
                                    for j in (EARLY[fq - 1], LATE[fq - 1]):
                                        if j is not None:
                                            with pe.If(n_next > j):
                                                pe.wait_ge(hBT_ready, first_next + (j + 1))
                            for j in range(DC):
                                last = pe.transpose(tb[:, j * P:(j + 1) * P], g1s[b % 2][:, j * P:(j + 1) * P],
                                                    ident[:, :])
                            last.then_inc(hid_full, 1)

                        def down(b):
                            pe.wait_ge(hidT_ready, k0 + (b + 1))
                            if fq == 0:
                                pe.wait_ge(y_added, beyond(first))
                            for j in range(DC):
                                last = three(oacc[b], hidT[b % 2], W2[u], lambda z: z[:, j, :],
                                             lambda z: z[:, j, :], fq == 0 and j == 0, fq == FQ - 1 and j == DC - 1)
                            last.then_inc(g2_done, 1)

                        def step(b):
                            if fq == 0:
                                pe.wait_ge(hBT_ready, first + (b + 1))
                            pe.wait_ge(g1_out, beyond(k0 + (b - 1)))
                            up(odd, u, b, range(DC))
                            turn(b - 1)
                            if b == 2:
                                pe.wait_ge(w2_ready, e * FQ + (fq + 1))
                            if b >= 2:
                                down(b - 2)

                        ends = fq == FQ - 1

                        def next_up_half_1():
                            pe.wait_ge(w1_ready, e * FQ + (fq + 2))
                            pe.wait_ge(g1_out, beyond(k0 + n))
                            if ends:
                                pe.wait_ge(hBT_ready, first_next + 1)
                            up(1 - odd if ends else odd, 1 - u, 0, range(DC // 2))

                        def next_up_half_2():
                            up(1 - odd if ends else odd, 1 - u, 0, range(DC // 2, DC))

                        for b in range(1, NB):
                            per_block(pe, n, b, step)
                        unless_last(pe, it, odd == 1 and ends, next_up_half_1)
                        for b in range(NB):
                            with pe.If(n == b + 1):
                                turn(b)
                        unless_last(pe, it, odd == 1 and ends, next_up_half_2)
                        if EARLY[fq] is not None:
                            with pe.If(n_next > EARLY[fq]):
                                prepare(first_next, EARLY[fq], k0 + n)
                        for b in range(NB):
                            with pe.If(n == b + 1):
                                if b < 2:
                                    pe.wait_ge(w2_ready, e * FQ + (fq + 1))
                                if b >= 1:
                                    down(b - 1)
                                down(b)
                        if LATE[fq] is not None:
                            with pe.If(n_next > LATE[fq]):
                                prepare(first_next, LATE[fq], k0 + n)


_INS = ["x", "ctx_1024", "fside_BxS2_0", "mask_BxS2_bk0", "g_xattn", "g_ffn", "L0_xattn_Wq_w", "L0_xattn_Wq_b",
        "L0_xattn_Wkv_w", "L0_xattn_Wkv_b", "L0_xattn_out_w", "L0_xattn_out_b", "L0_ffn_gate_w", "L0_ffn_gate_b",
        "L0_ffn_w1", "L0_ffn_b1", "L0_ffn_w2", "L0_ffn_b2"]


def kernel(**inputs):
    import numpy as _np
    import concourse.bacc as _bacc
    from concourse import mybir as _mybir
    from concourse.bass_utils import run_bass_kernel_spmd as _run

    nc = _bacc.Bacc("TRN2", target_bir_lowering=False, num_devices=1)
    arrays, args = {}, []
    for name in _INS:
        a = _np.ascontiguousarray(inputs[name])
        arrays[f"in_{name}_dram"] = a
        dt = U8 if a.dtype == _np.bool_ else _mybir.dt.from_np(a.dtype)
        args.append(nc.dram_tensor(f"in_{name}_dram", a.shape, dt, kind="ExternalInput").ap())
    out = nc.dram_tensor("out_0_dram", (BATCH, SEQ, D), F32, kind="ExternalOutput").ap()
    flamingo_block(nc, *args, out)
    r = _run(nc, [arrays], core_ids=[0])
    return r.results[0]["out_0_dram"]
```
